# Optimizing a Trainium2 kernel written in Bass

```python
import numpy as np
import jax
import jax.numpy as jnp

def _softmax(x, axis=-1):
    return jax.nn.softmax(x, axis=axis)

def _gelu(x):
    return jax.nn.gelu(x, approximate=True)

def _silu(x):
    return jax.nn.silu(x)

def _sigmoid(x):
    return jax.nn.sigmoid(x)

def _layernorm(x, axis=-1, eps=1e-05):
    m = jnp.mean(x, axis=axis, keepdims=True)
    v = jnp.var(x, axis=axis, keepdims=True)
    return (x - m) / jnp.sqrt(v + eps)

def _scatter_add(tgt, idx, src, axis=0):
    return tgt.at[idx].add(src)

def _segment_sum(src, seg, n):
    return jax.ops.segment_sum(src, seg, n)
kernel_name = 'mk_conv_preact_d4_conv_nchw128_r2_cf0417'

def setup_inputs(seed: int=0):
    np.random.seed(seed)
    _w = jnp.asarray

    def _rec_inputs():
        import jax
        import jax.numpy as jnp
        _gk = jax.random.key(seed)
        x = -7.109e-05 + 0.9999 * jax.random.normal(jax.random.fold_in(_gk, 1), (4, 64, 128, 128), jnp.float32)
        return x
    x = _rec_inputs()

    def _L0_conv_setup():
        import jax, jax.numpy as jnp
        import numpy as np
        C = 64
        GROUPS = 8
        EPS = 1e-05
        key = jax.random.key(seed)
        ks = jax.random.split(key, 7)
        x = jax.random.normal(ks[0], (8, C, 128, 128), dtype=jnp.float32)
        gn_w = jax.random.normal(ks[1], (C,), dtype=jnp.float32) * 0.02 + 1.0
        gn_b = jax.random.normal(ks[2], (C,), dtype=jnp.float32) * 0.02
        w1 = jax.random.normal(ks[3], (C, C), dtype=jnp.float32) * (1.0 / np.sqrt(C))
        b1 = jax.random.normal(ks[4], (C,), dtype=jnp.float32) * 0.02
        w2 = jax.random.normal(ks[5], (C, C), dtype=jnp.float32) * (1.0 / np.sqrt(C))
        b2 = jax.random.normal(ks[6], (C,), dtype=jnp.float32) * 0.02
        return {'x': x, 'gn_w': gn_w, 'gn_b': gn_b, 'w1': w1, 'b1': b1, 'w2': w2, 'b2': b2}
    _L0_conv_all = _L0_conv_setup()
    _L0_conv_in = {k: v for k, v in _L0_conv_all.items() if k in ('gn_w', 'gn_b', 'w1', 'b1', 'w2', 'b2')}
    del _L0_conv_all

    def _L1_conv_setup():
        import jax, jax.numpy as jnp
        import numpy as np
        import math
        C = 64
        KSIZE = 9
        PAD = KSIZE // 2

        def _conv1d(v, w, b):
            y = jax.lax.conv_general_dilated(v, w, window_strides=(1,), padding=[(PAD, PAD)], dimension_numbers=('NCH', 'OIH', 'NCH'))
            return y + b[None, :, None]

        def _sweep(x, w, b, axis, reverse):
            rows = jnp.moveaxis(x, axis, 0)
            if reverse:
                rows = rows[::-1]

            def step(prev, row):
                new = row + jax.nn.relu(_conv1d(prev, w, b))
                return (new, new)
            _, rest = jax.lax.scan(step, rows[0], rows[1:])
            out = jnp.concatenate([rows[:1], rest], axis=0)
            if reverse:
                out = out[::-1]
            return jnp.moveaxis(out, 0, axis)
        key = jax.random.key(seed)
        ks = jax.random.split(key, 9)
        B, H, W = (32, 36, 100)
        bound = math.sqrt(2.0 / (C * 9 * 5))
        x = jax.random.normal(ks[0], (B, C, H, W), dtype=jnp.float32)

        def wgt(k):
            return jax.random.uniform(k, (C, C, KSIZE), dtype=jnp.float32, minval=-bound, maxval=bound)

        def bia(k):
            return 0.01 * jax.random.normal(k, (C,), dtype=jnp.float32)
        return {'x': x, 'w_d': wgt(ks[1]), 'b_d': bia(ks[2]), 'w_u': wgt(ks[3]), 'b_u': bia(ks[4]), 'w_r': wgt(ks[5]), 'b_r': bia(ks[6]), 'w_l': wgt(ks[7]), 'b_l': bia(ks[8])}
    _L1_conv_all = _L1_conv_setup()
    _L1_conv_in = {k: v for k, v in _L1_conv_all.items() if k in ('w_d', 'b_d', 'w_u', 'b_u', 'w_r', 'b_r', 'w_l', 'b_l')}
    del _L1_conv_all

    def _L2_conv_setup():
        import jax, jax.numpy as jnp
        import numpy as np
        from jax import lax
        B, C, H, W = (16, 64, 32, 80)
        KW, KH = (9, 9)
        PAD_W, PAD_H = ((KW - 1) // 2, (KH - 1) // 2)

        def _slice_conv(s, K, pad):
            kern = jnp.transpose(K[:, 0], (0, 2, 1))
            y = lax.conv_general_dilated(jnp.swapaxes(s, 1, 2), kern, (1,), [(pad, pad)])
            return jnp.swapaxes(y, 1, 2)

        def _sweep(x, K, pad, reverse):
            if reverse:
                x = x[:, ::-1]
            xs = jnp.swapaxes(x, 0, 1)

            def step(prev, xi):
                new = xi + jax.nn.relu(_slice_conv(prev, K, pad))
                return (new, new)
            _, rest = lax.scan(step, xs[0], xs[1:])
            out = jnp.swapaxes(jnp.concatenate([xs[:1], rest], axis=0), 0, 1)
            if reverse:
                out = out[:, ::-1]
            return out
        key = jax.random.key(seed)
        kx, k1, k2, k3, k4 = jax.random.split(key, 5)
        bw = 1.0 / float(np.sqrt(KW * C))
        bh = 1.0 / float(np.sqrt(KH * C))
        x = jax.random.normal(kx, (B, C, H, W), jnp.float32)
        kernel_td = jax.random.uniform(k1, (C, 1, KW, C), jnp.float32, -bw, bw)
        kernel_dt = jax.random.uniform(k2, (C, 1, KW, C), jnp.float32, -bw, bw)
        kernel_lr = jax.random.uniform(k3, (C, 1, KH, C), jnp.float32, -bh, bh)
        kernel_rl = jax.random.uniform(k4, (C, 1, KH, C), jnp.float32, -bh, bh)
        return {'x': x, 'kernel_td': kernel_td, 'kernel_dt': kernel_dt, 'kernel_lr': kernel_lr, 'kernel_rl': kernel_rl}
    _L2_conv_all = _L2_conv_setup()
    _L2_conv_in = {k: v for k, v in _L2_conv_all.items() if k in ('kernel_td', 'kernel_dt', 'kernel_lr', 'kernel_rl')}
    del _L2_conv_all

    def _L3_conv_setup():
        import jax, jax.numpy as jnp
        import numpy as np
        MIDC = 64
        HEADS = 8
        HEADC = MIDC // HEADS
        EPS = 1e-05

        def _layernorm(t, w, b):
            mean = t.mean(-1, keepdims=True)
            std = jnp.std(t, axis=-1, ddof=1, keepdims=True)
            return w * ((t - mean) / (std + EPS)) + b
        key = jax.random.key(seed)
        ks = jax.random.split(key, 7)
        B, C, H, W = (8, MIDC, 64, 64)
        x = jax.random.normal(ks[0], (B, C, H, W), dtype=jnp.float32)
        s = 1.0 / np.sqrt(C)
        qkv_w = jax.random.normal(ks[1], (3 * C, C), dtype=jnp.float32) * s
        qkv_b = jnp.zeros((3 * C,), dtype=jnp.float32)
        o1_w = jax.random.normal(ks[2], (C, C), dtype=jnp.float32) * s
        o1_b = jnp.zeros((C,), dtype=jnp.float32)
        o2_w = jax.random.normal(ks[3], (C, C), dtype=jnp.float32) * s
        o2_b = jnp.zeros((C,), dtype=jnp.float32)
        kln_w = jnp.ones((HEADS, 1, HEADC), dtype=jnp.float32)
        kln_b = jnp.zeros((HEADS, 1, HEADC), dtype=jnp.float32)
        vln_w = jnp.ones((HEADS, 1, HEADC), dtype=jnp.float32)
        vln_b = jnp.zeros((HEADS, 1, HEADC), dtype=jnp.float32)
        return {'x': x, 'qkv_w': qkv_w, 'qkv_b': qkv_b, 'o1_w': o1_w, 'o1_b': o1_b, 'o2_w': o2_w, 'o2_b': o2_b, 'kln_w': kln_w, 'kln_b': kln_b, 'vln_w': vln_w, 'vln_b': vln_b}
    _L3_conv_all = _L3_conv_setup()
    _L3_conv_in = {k: v for k, v in _L3_conv_all.items() if k in ('qkv_w', 'qkv_b', 'o1_w', 'o1_b', 'o2_w', 'o2_b', 'kln_w', 'kln_b', 'vln_w', 'vln_b')}
    del _L3_conv_all
    return {'x': x, 'L0_conv_gn_w': _L0_conv_in['gn_w'], 'L0_conv_gn_b': _L0_conv_in['gn_b'], 'L0_conv_w1': _L0_conv_in['w1'], 'L0_conv_b1': _L0_conv_in['b1'], 'L0_conv_w2': _L0_conv_in['w2'], 'L0_conv_b2': _L0_conv_in['b2'], 'L1_conv_w_d': _L1_conv_in['w_d'], 'L1_conv_b_d': _L1_conv_in['b_d'], 'L1_conv_w_u': _L1_conv_in['w_u'], 'L1_conv_b_u': _L1_conv_in['b_u'], 'L1_conv_w_r': _L1_conv_in['w_r'], 'L1_conv_b_r': _L1_conv_in['b_r'], 'L1_conv_w_l': _L1_conv_in['w_l'], 'L1_conv_b_l': _L1_conv_in['b_l'], 'L2_conv_kernel_td': _L2_conv_in['kernel_td'], 'L2_conv_kernel_dt': _L2_conv_in['kernel_dt'], 'L2_conv_kernel_lr': _L2_conv_in['kernel_lr'], 'L2_conv_kernel_rl': _L2_conv_in['kernel_rl'], 'L3_conv_qkv_w': _L3_conv_in['qkv_w'], 'L3_conv_qkv_b': _L3_conv_in['qkv_b'], 'L3_conv_o1_w': _L3_conv_in['o1_w'], 'L3_conv_o1_b': _L3_conv_in['o1_b'], 'L3_conv_o2_w': _L3_conv_in['o2_w'], 'L3_conv_o2_b': _L3_conv_in['o2_b'], 'L3_conv_kln_w': _L3_conv_in['kln_w'], 'L3_conv_kln_b': _L3_conv_in['kln_b'], 'L3_conv_vln_w': _L3_conv_in['vln_w'], 'L3_conv_vln_b': _L3_conv_in['vln_b']}

def reference(x, L0_conv_gn_w, L0_conv_gn_b, L0_conv_w1, L0_conv_b1, L0_conv_w2, L0_conv_b2, L1_conv_w_d, L1_conv_b_d, L1_conv_w_u, L1_conv_b_u, L1_conv_w_r, L1_conv_b_r, L1_conv_w_l, L1_conv_b_l, L2_conv_kernel_td, L2_conv_kernel_dt, L2_conv_kernel_lr, L2_conv_kernel_rl, L3_conv_qkv_w, L3_conv_qkv_b, L3_conv_o1_w, L3_conv_o1_b, L3_conv_o2_w, L3_conv_o2_b, L3_conv_kln_w, L3_conv_kln_b, L3_conv_vln_w, L3_conv_vln_b):
    import jax
    import jax.numpy as jnp

    def _L0_conv_ref(x, gn_w, gn_b, w1, b1, w2, b2):
        import jax, jax.numpy as jnp
        import numpy as np
        C = 64
        GROUPS = 8
        EPS = 1e-05
        x_ifft = jnp.fft.ifft2(jnp.fft.fft2(x, axes=(-2, -1)), axes=(-2, -1)).real.astype(x.dtype)
        B, Ch, H, W = x_ifft.shape
        g = x_ifft.reshape(B, GROUPS, Ch // GROUPS, H, W)
        mean = g.mean(axis=(2, 3, 4), keepdims=True)
        var = g.var(axis=(2, 3, 4), keepdims=True)
        xn = ((g - mean) * jax.lax.rsqrt(var + EPS)).reshape(B, Ch, H, W)
        xn = xn * gn_w[None, :, None, None] + gn_b[None, :, None, None]
        h = jnp.einsum('oc,bchw->bohw', w1, xn) + b1[None, :, None, None]
        h = jax.nn.relu(h)
        ffn = jnp.einsum('oc,bchw->bohw', w2, h) + b2[None, :, None, None]
        return x_ifft + ffn

    def _L1_conv_ref(x, w_d, b_d, w_u, b_u, w_r, b_r, w_l, b_l):
        import jax, jax.numpy as jnp
        import numpy as np
        import math
        C = 64
        KSIZE = 9
        PAD = KSIZE // 2

        def _conv1d(v, w, b):
            y = jax.lax.conv_general_dilated(v, w, window_strides=(1,), padding=[(PAD, PAD)], dimension_numbers=('NCH', 'OIH', 'NCH'))
            return y + b[None, :, None]

        def _sweep(x, w, b, axis, reverse):
            rows = jnp.moveaxis(x, axis, 0)
            if reverse:
                rows = rows[::-1]

            def step(prev, row):
                new = row + jax.nn.relu(_conv1d(prev, w, b))
                return (new, new)
            _, rest = jax.lax.scan(step, rows[0], rows[1:])
            out = jnp.concatenate([rows[:1], rest], axis=0)
            if reverse:
                out = out[::-1]
            return jnp.moveaxis(out, 0, axis)
        out = _sweep(x, w_d, b_d, axis=2, reverse=False)
        out = _sweep(out, w_u, b_u, axis=2, reverse=True)
        out = _sweep(out, w_r, b_r, axis=3, reverse=False)
        out = _sweep(out, w_l, b_l, axis=3, reverse=True)
        return out

    def _L2_conv_ref(x, kernel_td, kernel_dt, kernel_lr, kernel_rl):
        import jax, jax.numpy as jnp
        import numpy as np
        from jax import lax
        B, C, H, W = (16, 64, 32, 80)
        KW, KH = (9, 9)
        PAD_W, PAD_H = ((KW - 1) // 2, (KH - 1) // 2)

        def _slice_conv(s, K, pad):
            kern = jnp.transpose(K[:, 0], (0, 2, 1))
            y = lax.conv_general_dilated(jnp.swapaxes(s, 1, 2), kern, (1,), [(pad, pad)])
            return jnp.swapaxes(y, 1, 2)

        def _sweep(x, K, pad, reverse):
            if reverse:
                x = x[:, ::-1]
            xs = jnp.swapaxes(x, 0, 1)

            def step(prev, xi):
                new = xi + jax.nn.relu(_slice_conv(prev, K, pad))
                return (new, new)
            _, rest = lax.scan(step, xs[0], xs[1:])
            out = jnp.swapaxes(jnp.concatenate([xs[:1], rest], axis=0), 0, 1)
            if reverse:
                out = out[:, ::-1]
            return out
        y = jnp.transpose(x, (0, 2, 3, 1))
        y = _sweep(y, kernel_td, PAD_W, False)
        y = _sweep(y, kernel_dt, PAD_W, True)
        y = jnp.swapaxes(y, 1, 2)
        y = _sweep(y, kernel_lr, PAD_H, False)
        y = _sweep(y, kernel_rl, PAD_H, True)
        y = jnp.swapaxes(y, 1, 2)
        return jnp.transpose(y, (0, 3, 1, 2))

    def _L3_conv_ref(x, qkv_w, qkv_b, o1_w, o1_b, o2_w, o2_b, kln_w, kln_b, vln_w, vln_b):
        import jax, jax.numpy as jnp
        import numpy as np
        MIDC = 64
        HEADS = 8
        HEADC = MIDC // HEADS
        EPS = 1e-05

        def _layernorm(t, w, b):
            mean = t.mean(-1, keepdims=True)
            std = jnp.std(t, axis=-1, ddof=1, keepdims=True)
            return w * ((t - mean) / (std + EPS)) + b
        B, C, H, W = x.shape
        N = H * W
        bias0 = x
        xf = x.transpose(0, 2, 3, 1).reshape(B, N, C)
        qkv = xf @ qkv_w.T + qkv_b
        qkv = qkv.reshape(B, N, HEADS, 3 * HEADC).transpose(0, 2, 1, 3)
        q, k, v = jnp.split(qkv, 3, axis=-1)
        k = _layernorm(k, kln_w, kln_b)
        v = _layernorm(v, vln_w, vln_b)
        kv = jnp.einsum('bhnd,bhne->bhde', k, v) / N
        av = jnp.einsum('bhnd,bhde->bhne', q, kv)
        av = av.transpose(0, 2, 1, 3).reshape(B, H, W, C)
        ret = av.transpose(0, 3, 1, 2) + bias0
        rf = ret.transpose(0, 2, 3, 1)
        h1 = jax.nn.gelu(rf @ o1_w.T + o1_b, approximate=False)
        h2 = h1 @ o2_w.T + o2_b
        return h2.transpose(0, 3, 1, 2) + bias0

    def _gn(v, G=32, eps=1e-05):
        B_, C_, H_, W_ = v.shape
        g = v.reshape(B_, G, C_ // G, H_, W_)
        m = jnp.mean(g, axis=(2, 3, 4), keepdims=True)
        s = jnp.var(g, axis=(2, 3, 4), keepdims=True)
        return ((g - m) / jnp.sqrt(s + eps)).reshape(v.shape)

    def _ln_c(v, eps=1e-06):
        m = jnp.mean(v, axis=1, keepdims=True)
        s = jnp.var(v, axis=1, keepdims=True)
        return (v - m) / jnp.sqrt(s + eps)

    def _ln_t(v, eps=1e-05):
        m = jnp.mean(v, axis=-1, keepdims=True)
        s = jnp.var(v, axis=-1, keepdims=True)
        return (v - m) / jnp.sqrt(s + eps)

    def _to_tokens(v):
        B_, C_, H_, W_ = v.shape
        return v.reshape(B_, C_, H_ * W_).transpose(0, 2, 1)

    def _from_tokens(t, like):
        B_, C_, H_, W_ = like.shape
        return t.transpose(0, 2, 1).reshape(B_, C_, H_, W_)
    x = x + _L0_conv_ref(_gn(x), L0_conv_gn_w, L0_conv_gn_b, L0_conv_w1, L0_conv_b1, L0_conv_w2, L0_conv_b2)
    x = x + _L1_conv_ref(_gn(x), L1_conv_w_d, L1_conv_b_d, L1_conv_w_u, L1_conv_b_u, L1_conv_w_r, L1_conv_b_r, L1_conv_w_l, L1_conv_b_l)
    x = x + _L2_conv_ref(_gn(x), L2_conv_kernel_td, L2_conv_kernel_dt, L2_conv_kernel_lr, L2_conv_kernel_rl)
    x = x + _L3_conv_ref(_gn(x), L3_conv_qkv_w, L3_conv_qkv_b, L3_conv_o1_w, L3_conv_o1_b, L3_conv_o2_w, L3_conv_o2_b, L3_conv_kln_w, L3_conv_kln_b, L3_conv_vln_w, L3_conv_vln_b)
    return x

_drawn_inputs = setup_inputs


def setup_inputs(seed=0):
    import zlib

    import numpy as np

    out = dict(_drawn_inputs(seed))
    spreads = {'L3_conv_qkv_b': (0.0, 0.8),
     'L3_conv_o1_b': (0.0, 0.798),
     'L3_conv_o2_b': (0.0, 0.475),
     'L3_conv_kln_w': (1.0, 0.6),
     'L3_conv_kln_b': (0.0, 0.8),
     'L3_conv_vln_w': (1.0, 0.6),
     'L3_conv_vln_b': (0.0, 0.8)}
    factors = {'L0_conv_gn_w': 7.635,
     'L0_conv_gn_b': 23.511,
     'L0_conv_b1': 24.725,
     'L0_conv_b2': 6.998,
     'L1_conv_b_d': 54.942,
     'L1_conv_b_u': 59.715,
     'L1_conv_b_r': 47.293,
     'L1_conv_b_l': 51.228}
    for name, (base, spread) in spreads.items():
        noise = np.random.default_rng([zlib.crc32(name.encode()), seed]).standard_normal(out[name].shape)
        drawn = base * np.exp(spread * noise) if base else spread * noise
        out[name] = jnp.asarray(drawn.astype(out[name].dtype))
    for name, factor in factors.items():
        out[name] = (out[name] * factor).astype(out[name].dtype)
    return out
```

```python
import numpy as np
import concourse.bass as bass
from concourse import mybir
from contextlib import ExitStack

STOP = 99


def build_program(nc, D, out, debug):
    F32, F32R = mybir.dt.float32, mybir.dt.float32r
    ALU, ACT, AX = mybir.AluOpType, mybir.ActivationFunctionType, mybir.AxisListType
    B, C, H, W = 4, 64, 128, 128
    P = 2 * C
    HALF = W // 2
    ROW = B * HALF
    PAIRS = H // 2
    TAPS2 = 5
    PADDED = HALF + 4
    CR = 8
    CHUNKS = H // CR
    NT = CR * HALF
    RING = 4
    EPS = 1e-5
    HEADS, HD = 8, 8
    GROUPS = 8 * 2 * HEADS
    N_PIX = H * W

    sweeps = []
    for layer in (0, 1):
        sweeps += [(layer, "H", False), (layer, "H", True), (layer, "W", False), (layer, "W", True)]
    NS = len(sweeps)
    LIM = NS if STOP >= 2 else 4 if STOP >= 1 else 1

    ctx = ExitStack()
    with ctx:
        def sb(name, shape, dt=F32):
            return ctx.enter_context(nc.sbuf_tensor(name, shape, dt))

        def sem(name):
            return ctx.enter_context(nc.semaphore(name))

        state = sb("state", [P, H, B, HALF])
        state_b = state[:].rearrange("p (hp s) b w -> p hp s b w", s=2)
        res = sb("res", [P, RING, CR, ROW])
        x_row = [[sb(f"x_row{c}{k}", [P, 2, PADDED]) for k in range(2)] for c in range(2)]
        biased_row = sb("biased_row", [P, 2, B, HALF])
        turn_ring = sb("turn_ring", [P, 2, 2, B, HALF])
        w_taps = sb("w_taps", [P, 2, TAPS2, P])
        sweep_bias = sb("sweep_bias", [P, NS])
        sweep_nbias = sb("sweep_nbias", [P, NS])
        gmats = sb("gmats", [P, 2, P])
        vecs = sb("vecs", [P, 6])
        stats = sb("stats", [P, B, CHUNKS, 6])
        mv = sb("mv", [P, B, 2])
        gn_mean = sb("gn_mean", [P, B])
        gn_var = sb("gn_var", [P, B])
        gn_a = sb("gn_a", [P, B])
        gn_c = sb("gn_c", [P, B])
        gn_t = sb("gn_t", [P, 4, B])
        a1 = sb("a1", [P, B])
        cb = sb("cb", [P, B])
        aff = sb("aff", [P, 2, B])
        eps_t = sb("eps_t", [P, 1])
        ffn1_w = sb("ffn1_w", [P, P])
        ffn2_w = sb("ffn2_w", [P, 2, P])
        ffn1_s = sb("ffn1_s", [P, B, P])
        ffn1_b = sb("ffn1_b", [P, B])
        hid = sb("hid", [P, 2, NT])
        ring = [0, res[:].rearrange("p a r c -> p (a r c)")]

        def in_ring(n):
            ring[0] += n
            assert ring[0] <= RING * CR * ROW
            return ring[1][:, ring[0] - n:ring[0]]

        def slots(ap):
            return ap.rearrange("p (k n) -> p k n", k=2)

        y_st = slots(in_ring(2 * NT))
        sq = slots(in_ring(4 * NT))
        gram_k = slots(in_ring(2 * NT))
        gram_v = slots(in_ring(2 * NT))
        ssum = slots(in_ring(2 * GROUPS))
        sdev = slots(in_ring(2 * GROUPS))
        dev = slots(in_ring(2 * GROUPS))
        rinv = slots(in_ring(2 * GROUPS))
        rkv = slots(in_ring(GROUPS))
        gram_sb = sq[:, 0, 0:4 * P].rearrange("p (b n) -> p b n", b=B)
        t1_sb = sq[:, 0, 4 * P:4 * P + B * C]
        kvt_sb = sq[:, 0, 4 * P + B * C:4 * P + 2 * B * C].rearrange("p (b n) -> p b n", b=B)
        ht_sb = sq[:, 1, 0:B * C]
        gt_sb = sq[:, 1, B * C:2 * B * C].rearrange("p (b n) -> p b n", b=B)
        ht_dup = sq[:, 1, 2 * B * C:4 * B * C].rearrange("p (b r n) -> p b r n", b=B, r=2)
        gt_dup = y_st[:, 0, :].rearrange("p (b r n) -> p b r n", b=B, r=2)
        kv_w = sb("kv_w", [P, 2 * P])
        bias_raw = sb("bias_raw", [C, P])
        bias_hi = sb("bias_hi", [C, P], F32R)
        bias_rows = sb("bias_rows", [P, 4, P], F32R)
        ones = sb("ones", [P, P], F32R)
        centre = sb("centre", [P, 32])
        ln_rows = sb("ln_rows", [P, 4, C])
        ln_pat = sb("ln_pat", [P, 2, C])
        uv = sb("uv", [P, 2, C])
        uv_t = sb("uv_t", [P, 2, C])
        gmask = sb("gmask", [P, P])
        wq_dup = sb("wq_dup", [C, 2, C])
        o1_t = sb("o1_t", [P, C])
        bq = sb("bq", [C, 1])

        BANK = 512
        pair = [ctx.enter_context(nc.psum_tensor(f"banks{2 * i}_{2 * i + 1}", [P, 2 * BANK], F32)) for i in range(4)]
        bank = [pair[i // 2][:, (i % 2) * BANK:(i % 2 + 1) * BANK] for i in range(8)]

        resid = D["resid"]

        s_x = [sem(f"s_x{j}") for j in range(CHUNKS)]
        s_const = sem("s_const")
        s_set = sem("s_set")
        s_gp = sem("s_gp")
        s_gq = sem("s_gq")
        s_sq = sem("s_sq")
        s_rt = sem("s_rt")
        s_dve = sem("s_dve")
        s_coef = sem("s_coef")
        s_up = sem("s_up")
        s_act = sem("s_act")
        s_xs = sem("s_xs")
        s_dn = sem("s_dn")
        s_sum = sem("s_sum")
        s_h = [sem(f"s_h{c}") for c in range(2)]
        s_new = [sem(f"s_new{c}") for c in range(2)]
        s_conv = [sem(f"s_conv{c}") for c in range(2)]
        s_row = sem("s_row")
        s_w = [sem(f"s_w{k}") for k in range(2)]
        s_turn = [sem(f"s_turn{k}") for k in range(2)]
        s_rst = sem("s_rst")
        s_rst1 = [sem(f"s_rst1_{j}") for j in range(CHUNKS)]
        s_rld = [sem(f"s_rld{k}") for k in range(RING)]
        s_add = sem("s_add")
        s_cross = sem("s_cross")
        s_out = sem("s_out")
        s_y = sem("s_y")
        s_kv = sem("s_kv")
        s_sqr = sem("s_sqr")
        s_kc = sem("s_kc")
        s_ss = sem("s_ss")
        s_sd = sem("s_sd")
        s_dv = sem("s_dv")
        s_ri = sem("s_ri")
        s_vs = sem("s_vs")
        s_tl = sem("s_tl")
        s_gr = sem("s_gr")
        s_k3 = sem("s_k3")
        s_k3l = sem("s_k3l")

        block = ctx.enter_context(nc.Block())

        STEPS = H - 1

        def hbase(n):
            return sum(STEPS + (0 if rev else 1) for _, _, rev in sweeps[:n])

        def row_count(n):
            return sum(STEPS + (0 if (m % 4 == 3) else 1) for m in range(n))

        def row_of(rev, i, k):
            return (H - 1 - k) - 2 * i if rev else 2 * i + k

        def cells(n, c, i, k):
            _, along, rev = sweeps[n]
            r = row_of(rev, i, k)
            if along == "H":
                return state[:, r, 2 * c:2 * c + 2, :]
            s = (1 - k) if rev else k
            wp = (HALF - 1) - i if rev else i
            return state_b[:, :, s, 2 * c:2 * c + 2, wp].rearrange("p h b -> p b h")

        def slot(n, k):
            return (k + 1) % 2 if sweeps[n][2] else k

        @block.sync
        def _(sp):
            for j in range(CHUNKS):
                sp.dma_start(state[:, j * CR:(j + 1) * CR, :, :], D["x"][:, j * CR:(j + 1) * CR, :]
                             .rearrange("p r (b w) -> p r b w", b=B)).then_inc(s_x[j], 16)

            def store_residual_a(j):
                for q in range(2):
                    for r in range(2):
                        src = state[q * C:(q + 1) * C, :, :, :].rearrange(
                            "c (j hp r) b w -> c j hp r (b w)", r=2, hp=CR // 2)[:, j, :, r, :]
                        dst = resid.rearrange("(j hp) (r c) s n -> j r c s hp n", hp=CR // 2, r=2)[j, r, :, q, :, :]
                        sp.dma_start(dst, src).then_inc(s_rst, 16)

            with sp.Fori(0, CHUNKS) as j:
                sp.wait_ge(s_sum, j * B + B)
                store_residual_a(j)

            def dump():
                sp.dma_start(out[:, :], state[:].rearrange("p r b w -> p (r b w)")).then_inc(s_out, 16)
                sp.wait_ge(s_out, 16)
            if STOP < 1:
                sp.wait_ge(s_sum, B * CHUNKS)
                dump()
                return
            for layer in (0, 1):
                n = 4 * layer + 1
                sp.wait_ge(s_new[0], STEPS * n + 1)
                sp.wait_ge(s_new[1], STEPS * n + 1)
                sp.wait_ge(s_row, row_count(n) + 2)

                def turn(m, k):
                    hp = m * -2 + (PAIRS - 1 - k)
                    for s in range(2):
                        for q in range(2):
                            sp.dma_start(state_b[q * C:(q + 1) * C, hp, s, :, :],
                                         turn_ring[s * C:(s + 1) * C, k, q, :, :]).then_inc(s_turn[k], 16)
                turn(0, 0)
                sp.wait_ge(s_new[0], STEPS * n + 3)
                sp.wait_ge(s_new[1], STEPS * n + 3)
                turn(0, 1)
                with sp.Fori(1, PAIRS // 2) as m:
                    for k in range(2):
                        sp.wait_ge(s_new[0], m * 4 + (STEPS * n + 2 * k + 1))
                        sp.wait_ge(s_new[1], m * 4 + (STEPS * n + 2 * k + 1))
                        turn(m, k)
                if STOP < 2:
                    sp.wait_ge(s_new[0], STEPS * 4)
                    sp.wait_ge(s_new[1], STEPS * 4)
                    dump()
                    return
                if layer == 0:
                    sp.wait_ge(s_rst, 16 * 4 * CHUNKS)
                else:
                    for j in range(CHUNKS):
                        sp.wait_ge(s_rst1[j], 16)
                for j in range(CHUNKS):
                    if j >= RING:
                        sp.wait_ge(s_add, layer * CHUNKS + j - RING + 1)
                    sp.dma_start(res[:, j % RING, :, :].rearrange("p (hp s) n -> p hp (s n)", s=2),
                                 resid.rearrange("hp p s n -> p hp (s n)")[:, j * CR // 2:(j + 1) * CR // 2, :]
                                 ).then_inc(s_rld[j % RING], 16)
                if layer == 0:
                    for j in range(CHUNKS):
                        sp.wait_ge(s_add, j + 1)
                        sp.wait_ge(s_rld[j % RING], 16 * (j // RING + 1))
                        sp.dma_start(resid.rearrange("hp p s n -> p hp (s n)")[:, j * CR // 2:(j + 1) * CR // 2, :],
                                     state[:, j * CR:(j + 1) * CR, :, :].rearrange("p (hp s) b w -> p hp (s b w)", s=2)
                                     ).then_inc(s_rst1[j], 16)
                    for j in range(CHUNKS):
                        sp.wait_ge(s_rst1[j], 16)
                        sp.wait_ge(s_sum, CHUNKS * B + j + 1)
                        for q in range(2):
                            sp.dma_start(state_b[q * C:(q + 1) * C, j * CR // 2:(j + 1) * CR // 2, 1 - q, :, :],
                                         resid.rearrange("hp (r c) s (b w) -> r c hp s b w", r=2, b=B)
                                         [1 - q, :, j * CR // 2:(j + 1) * CR // 2, q, :, :]).then_inc(s_cross, 16)
            if STOP < 3:
                sp.wait_ge(s_sum, B * CHUNKS + 2 * CHUNKS)
                dump()
                return
            with sp.Fori(0, CHUNKS) as j:
                sp.wait_ge(s_sum, j * B + (B * CHUNKS + 2 * CHUNKS + B))
                sp.dma_start(out[:, bass.ts(j, CR * ROW)], state[:].rearrange("p (j r) b w -> p j (r b w)", r=CR)[:, j, :]
                             ).then_inc(s_out, 16)
            sp.wait_ge(s_out, 16 * CHUNKS)

        @block.gpsimd
        def _(pool):
            nc.gpsimd.memset(eps_t[:], EPS).then_inc(s_set, 1)
            nc.gpsimd.memset(w_taps[:], 0.0).then_inc(s_set, 1)
            nc.gpsimd.memset(ffn1_w[:], 0.0).then_inc(s_set, 1)
            nc.gpsimd.memset(ffn2_w[:], 0.0).then_inc(s_set, 1)
            for c in range(2):
                for k in range(2):
                    nc.gpsimd.memset(x_row[c][k][:], 0.0).then_inc(s_set, 1)
            nc.gpsimd.memset(kv_w[:], 0.0).then_inc(s_set, 1)
            nc.gpsimd.memset(bias_raw[:], 0.0).then_inc(s_set, 1)
            nc.gpsimd.memset(bias_rows[:].bitcast(F32), 0.0).then_inc(s_set, 1)
            nc.gpsimd.memset(ones[:].bitcast(F32), 1.0).then_inc(s_set, 1)
            if STOP < 3:
                return

            def tails(b, n, started):
                k = b % 2
                pool.wait_ge(s_ri, n + 1)
                if started:
                    pool.wait_ge(s_gr, n - 1)
                for dst, src in ((gram_k, dev), (gram_v, rinv)):
                    last = nc.gpsimd.tensor_tensor(
                        dst[:, k, :].rearrange("p (g h e) -> p g h e", h=HEADS, e=HD)[:, :, :, HD - 1],
                        src[:, k, :].rearrange("p (g v h) -> p g v h", v=2, h=HEADS)[:, :, 0, :],
                        ones[:, 0:8 * HEADS].bitcast(F32).rearrange("p (g h) -> p g h", h=HEADS), ALU.mult)
                last.then_inc(s_tl, 1)

            for b in range(B):
                tails(b, b, b >= 2)
            with pool.Fori(1, CHUNKS) as j:
                for b in range(B):
                    tails(b, j * B + b, True)
        @block.scalar
        def _(act):
            act.wait_ge(s_set, 12)
            for dst, src in ((gmats[:], D["gmats"].rearrange("g p q -> p g q")), (vecs[:], D["vecs"]), (sweep_bias[:], D["sbias"])):
                act.dma_start(dst, src).then_inc(s_const, 16)
            for q in range(2):
                blk = slice(q * C, (q + 1) * C)
                act.dma_start(ffn1_w[blk, blk], D["w1t"]).then_inc(s_const, 16)
                act.dma_start(ffn2_w[blk, 0, blk], D["w2t"]).then_inc(s_const, 16)
                act.dma_start(ffn2_w[blk, 1, blk], D["o2t"]).then_inc(s_const, 16)

                act.dma_start(kv_w[blk, q * P:(q + 1) * P], D["kvt"]).then_inc(s_k3l, 16)
                act.dma_start(bias_raw[32 * q:32 * q + 1, :], D["kvb"]).then_inc(s_k3l, 16)
                act.dma_start(wq_dup[:, q, :], D["wq"]).then_inc(s_k3l, 16)
                act.dma_start(o1_t[blk, :], D["o1t"]).then_inc(s_k3l, 16)
            for dst, name in ((bq[:], "bq"), (ln_rows[:], "ln_rows"), (ln_pat[:], "ln_pat"), (gmask[:], "gmask")):
                act.dma_start(dst, D[name]).then_inc(s_k3l, 16)

            def load_taps(n):
                if n >= 2:
                    act.wait_ge(s_conv[1], STEPS * (n - 1))
                for q in range(2):
                    for r in range(2):
                        taps = [(s, 2 * s + q - r) for s in range(TAPS2) if 0 <= 2 * s + q - r <= 8]
                        s0, t0, cnt = taps[0][0], taps[0][1], len(taps)
                        act.dma_start(w_taps[q * C:(q + 1) * C, n % 2, s0:s0 + cnt, r * C:(r + 1) * C],
                                      D["taps"][n, :, t0:t0 + 2 * cnt - 1:2, :]).then_inc(s_w[n % 2], 16)

            load_taps(0)

            def root(k):
                act.wait_ge(s_sq, k)
                nc.scalar.activation(gn_t[:, 1, :], gn_t[:, 0, :], ACT.Sqrt, bias=eps_t[:]).then_inc(s_rt, 1)

            root(1)
            root(2)

            def ffn(layer, func):
                base = B * CHUNKS * layer
                sbase = B * CHUNKS + 2 * CHUNKS if layer else 0
                act.wait_ge(s_coef, 5 if layer else 1)
                def tile(j, b):
                    t = j * B + (b + base)
                    act.wait_ge(s_up, t + 1)
                    nc.scalar.activation(hid[:, b % 2, :], bank[b % 2], func, bias=ffn1_b[:, b:b + 1]).then_inc(s_act, 1)
                    xs = state[:, bass.ts(j, CR), b, :]
                    nc.scalar.activation(xs, xs, ACT.Identity, scale=a1[:, b:b + 1], bias=cb[:, b:b + 1]).then_inc(s_xs, 1)
                with act.Fori(0, CHUNKS) as j:
                    for b in range(B):
                        tile(j, b)

            ffn(0, ACT.Relu)
            if STOP < 1:
                return

            def rows(n):
                layer, along, rev = sweeps[n]
                first, start = n % 4 == 0, row_count(n)
                if n + 1 < LIM:
                    load_taps(n + 1)
                if first:
                    root(3 + layer)
                    act.wait_ge(s_coef, 2 + layer)
                    if layer == 0:
                        act.wait_ge(s_rst, 16 * 4 * CHUNKS)
                    else:
                        act.wait_ge(s_cross, 16 * 2 * CHUNKS)
                if n % 4 == 2:
                    for k in range(2):
                        act.wait_ge(s_turn[k], 64 * (PAIRS // 2) * (layer + 1))
                elif n % 4 != 0:
                    act.wait_ge(s_new[0], STEPS * n)
                    act.wait_ge(s_new[1], STEPS * n)

                def row(i, k):
                    if first:
                        for b in range(B):
                            src = state[:, row_of(rev, i, k), b, :]
                            last = nc.scalar.activation(biased_row[:, k, b, :], src, ACT.Identity,
                                                        scale=gn_a[:, b:b + 1], bias=aff[:, 0, b:b + 1])
                        last.then_inc(s_row, 1)
                        return
                    if along == "H":
                        src = state[:, row_of(rev, i, k), :, :]
                    else:
                        s = (1 - k) if rev else k
                        src = state_b[:, :, s, :, (HALF - 1) - i if rev else i].rearrange("p h b -> p b h")
                    nc.scalar.activation(biased_row[:, k, :, :], src, ACT.Identity,
                                         bias=sweep_bias[:, n:n + 1]).then_inc(s_row, 1)

                if first:
                    for b in range(B):
                        xs = state[:, 0, b, :]
                        last = nc.scalar.activation(xs, xs, ACT.Identity, scale=gn_a[:, b:b + 1], bias=gn_c[:, b:b + 1])
                    last.then_inc(s_row, 1)
                elif n % 4 == 1:
                    nc.scalar.activation(turn_ring[:, 0, 1, :, :], state[:, H - 1, :, :], ACT.Copy).then_inc(s_row, 1)
                elif n % 4 == 2:
                    nc.scalar.activation(biased_row[:, 0, :, :], state_b[:, :, 0, :, 0].rearrange("p h b -> p b h"),
                                         ACT.Copy).then_inc(s_row, 1)
                row(0, 1)

                def next_row(i, k):
                    for c in range(2):
                        act.wait_ge(s_h[c], i * 2 + (hbase(n) + k - 2 + (0 if rev else 1)))
                        if not isinstance(i, int) or STEPS * n + k:
                            act.wait_ge(s_new[c], i * 2 + (STEPS * n + k - 2))
                    row(i, k)

                if n == 0:
                    next_row(1, 0)
                    next_row(1, 1)
                with act.Fori(2 if n == 0 else 1, PAIRS) as i:
                    for k in range(2):
                        next_row(i, k)

            for n in range(4):
                rows(n)
            if STOP < 2:
                return
            for n in range(4, 8):
                rows(n)
            if STOP < 3:
                return
            root(5)
            act.wait_ge(s_coef, 4)

            def kv_root(k, n):
                act.wait_ge(s_ss, n + 1)
                nc.scalar.activation(sdev[:, k, :], ssum[:, k, :], ACT.Sqrt, scale=1.0 / (HD - 1)).then_inc(s_sd, 1)

            def kv_square(k, n, started):
                act.wait_ge(s_kv, n + 1)
                if started:
                    act.wait_ge(s_ss, n - 1)
                    act.wait_ge(s_gr, n - 1)
                nc.scalar.activation(sq[:, k, :], pair[k][:], ACT.Square).then_inc(s_sqr, 1)
                src = pair[k][:].rearrange("p (g v h e) -> p g v h e", v=2, h=HEADS, e=HD)[:, :, 0, :, 0:HD - 1]
                dst = gram_k[:, k, :].rearrange("p (g h e) -> p g h e", h=HEADS, e=HD)[:, :, :, 0:HD - 1]
                nc.scalar.activation(dst, src, ACT.Copy).then_inc(s_kc, 1)

            def kv_stage(j, b, started):
                n = j * B + b
                if started or b >= 2:
                    act.wait_ge(s_kv, n - 1)
                nc.scalar.activation(y_st[:, b % 2, :].rearrange("p (r w) -> p r w", r=CR), state[:, bass.ts(j, CR), b, :],
                                     ACT.Identity, scale=gn_a[:, b:b + 1], bias=gn_c[:, b:b + 1]).then_inc(s_y, 1)
                if started or b >= 2:
                    kv_root(b % 2, n - 2)
                if started or b >= 1:
                    kv_square((b + 1) % 2, n - 1, started or b >= 3)

            for b in range(B):
                kv_stage(0, b, False)
            with act.Fori(1, CHUNKS) as j:
                for b in range(B):
                    kv_stage(j, b, True)
            n = B * CHUNKS
            kv_root(0, n - 2)
            kv_square(1, n - 1, True)
            kv_root(1, n - 1)
            ffn(1, ACT.Gelu)

        @block.tensor
        def _(pe):
            steps = [0]

            def stat_product(g, cols):
                steps[0] += 1
                pe.wait_ge(s_gp, steps[0])
                nc.tensor.matmul(bank[7][:, 0:cols.shape[-1]], gmats[:, g, :], cols, start=True, stop=True).then_inc(s_gq, 1)

            pe.wait_ge(s_const, 16 * 9)
            stat_product(0, gn_t[:, 2, :])
            stat_product(0, gn_t[:, 3, :])
            stat_product(1, gn_t[:, 2, :])
            steps[0] += 1
            pe.wait_ge(s_gp, steps[0])
            nc.tensor.matmul(bank[7][:, 0:B], ffn1_w[:], aff[:, 1, :], start=True, stop=True).then_inc(s_gq, 1)

            def ffn(layer):
                base = B * CHUNKS * layer
                sbase = B * CHUNKS + 2 * CHUNKS if layer else 0
                pe.wait_ge(s_coef, 5 if layer else 1)

                def up(j, b):
                    nc.tensor.matmul(bank[b % 2], ffn1_s[:, b, :], state[:, bass.ts(j, CR), b, :],
                                     start=True, stop=True).then_inc(s_up, 1)

                def down(b):
                    nc.tensor.matmul(bank[2 + b % 2], ffn2_w[:, layer, :], hid[:, b % 2, :],
                                     start=True, stop=True).then_inc(s_dn, 1)

                def second(j, b, start):
                    pe.wait_ge(s_act, j * B + (base + b + 1))
                    if b >= 2 or not start:
                        pe.wait_ge(s_sum, j * B + (sbase + b - 1))
                    down(b)

                def chunk(j, start):
                    for b in range(B):
                        up(j, b)
                        if b:
                            second(j, b - 1, start)
                    second(j, B - 1, start)
                chunk(0, True)
                with pe.Fori(1, CHUNKS) as j:
                    chunk(j, False)

            ffn(0)
            if STOP < 1:
                return

            def conv(n, c, k, hcount):
                par, src = slot(n, k), slot(n, 1 - k)
                out_ps = bank[2 * c + par][:, 0:2 * HALF].rearrange("p (b w) -> p b w", b=2)
                pe.wait_ge(s_h[c], hcount)
                for s in range(TAPS2):
                    last = nc.tensor.matmul(out_ps, w_taps[:, n % 2, s, :], x_row[c][src][:, :, s:s + HALF],
                                            start=s == 0, stop=s == TAPS2 - 1)
                last.then_inc(s_conv[c], 1)

            def sweep(n):
                rev = sweeps[n][2]
                before = hbase(n) + (0 if rev else 1)
                pe.wait_ge(s_w[n % 2], 64 * (n // 2 + 1))
                for c in range(2):
                    conv(n, c, 1, before)
                with pe.Fori(1, PAIRS) as i:
                    for k in range(2):
                        for c in range(2):
                            conv(n, c, k, i * 2 + (before + k - 1))

            for n in range(NS if STOP >= 2 else 4):
                if n % 4 == 0:
                    stat_product(0, gn_t[:, 2, :])
                    stat_product(0, gn_t[:, 3, :])
                sweep(n)
            if STOP < 3:
                return
            stat_product(0, gn_t[:, 2, :])
            stat_product(0, gn_t[:, 3, :])

            def kv_products(j, b, started):
                k, n = b % 2, j * B + b
                pe.wait_ge(s_y, n + 1)
                if started or b >= 2:
                    pe.wait_ge(s_vs, n - 1)
                for u in range(2):
                    ps = pair[k][:, u * BANK:(u + 1) * BANK]
                    nc.tensor.matmul(ps, ones[:], bias_rows[:].rearrange("p r n -> p (r n)"), start=True, stop=False)
                    for t in range(2):
                        col = (2 * u + t) * P
                        last = nc.tensor.matmul(ps[:, t * 2 * P:(t + 1) * 2 * P], y_st[:, k, col:col + P], kv_w[:],
                                                start=False, stop=t == 1)
                last.then_inc(s_kv, 1)

            def gram(b, n, first, last_of_image):
                k = b % 2
                pe.wait_ge(s_vs, n + 1)
                pe.wait_ge(s_tl, n + 1)
                pe.wait_ge(s_kc, n + 1)
                for t in range(4):
                    blk = slice(t * P, (t + 1) * P)
                    last = nc.tensor.matmul(bank[4 + b][:, 0:P], gram_k[:, k, blk], gram_v[:, k, blk],
                                            start=first and t == 0, stop=last_of_image and t == 3)
                last.then_inc(s_gr, 1)

            for m in range(2 * B):
                kv_products(m // B, m % B, m >= B)
                if m >= 2:
                    gram((m - 2) % B, m - 2, m - 2 < B, False)
            with pe.Fori(2, CHUNKS - 1) as j:
                for b in range(B):
                    kv_products(j, b, True)
                    gram((b + 2) % B, j * B + (b - 2), False, False)
            for b in range(B + 2):
                n = B * (CHUNKS - 1) + b
                if b < B:
                    kv_products(CHUNKS - 1, b, True)
                gram((b + 2) % B, n - 2, False, b >= 2)

            def operands():
                steps[0] += 1
                pe.wait_ge(s_gp, steps[0])

            operands()
            for b in range(B):
                last = nc.tensor.matmul(bank[0][:, b * C:(b + 1) * C], gram_sb[:, b, :], uv[:, 0, :], start=True, stop=True)
            last.then_inc(s_gq, 1)
            operands()
            nc.tensor.matmul(bank[1][0:C, 0:B * C], uv[:, 1, :], t1_sb, start=True, stop=True).then_inc(s_gq, 1)
            operands()
            for b in range(B):
                last = nc.tensor.matmul(bank[2][0:C, b * C:(b + 1) * C], kvt_sb[0:C, b, :], o1_t[0:C, :], start=True, stop=True)
            last.then_inc(s_gq, 1)
            operands()
            nc.tensor.matmul(bank[3][:, 0:B * C], wq_dup[:].rearrange("p r n -> p (r n)"), ht_sb[0:C, :],
                             start=True, stop=True).then_inc(s_gq, 1)
            operands()
            for b in range(B):
                nc.tensor.matmul(bank[0][:, b:b + 1], gt_dup[0:C, b, :, :].rearrange("p r n -> p (r n)"), gn_c[0:C, b:b + 1],
                                 start=True, stop=False)
                last = nc.tensor.matmul(bank[0][:, b:b + 1], ht_dup[0:C, b, :, :].rearrange("p r n -> p (r n)"), bq[:],
                                        start=False, stop=True)
            last.then_inc(s_gq, 1)
            ffn(1)

        @block.vector
        def _(dve):
            chain = [0]

            def link(ins):
                chain[0] += 1
                ins.then_inc(s_dve, 1)
                dve.wait_ge(s_dve, chain[0])

            gp, gq, rt = [0], [0], [0]

            def to_pe(ins):
                ins.then_inc(s_gp, 1)
                gq[0] += 1
                dve.wait_ge(s_gq, gq[0])

            def rsqrt(dst, var):
                nc.vector.tensor_copy(gn_t[:, 0, :], var).then_inc(s_sq, 1)
                rt[0] += 1
                dve.wait_ge(s_rt, rt[0])
                link(nc.vector.reciprocal(dst, gn_t[:, 1, :]))

            def group_norm():
                for b in range(B):
                    ins = nc.vector.bn_aggr(mv[:, b, :], stats[:, b, :, :].rearrange("p j s -> p (j s)"))
                link(ins)
                to_pe(nc.vector.tensor_copy(gn_t[:, 2, :], mv[:, :, 0]))
                link(nc.vector.tensor_copy(gn_mean[:], bank[7][:, 0:B]))
                link(nc.vector.tensor_tensor(gn_t[:, 0, :], mv[:, :, 0], gn_mean[:], ALU.subtract))
                link(nc.vector.tensor_tensor(gn_t[:, 0, :], gn_t[:, 0, :], gn_t[:, 0, :], ALU.mult))
                to_pe(nc.vector.tensor_tensor(gn_t[:, 3, :], gn_t[:, 0, :], mv[:, :, 1], ALU.add))
                link(nc.vector.tensor_copy(gn_var[:], bank[7][:, 0:B]))
                rsqrt(gn_a[:], gn_var[:])
                link(nc.vector.scalar_tensor_tensor(gn_c[:], gn_mean[:], -1.0, gn_a[:], ALU.mult, ALU.mult))

            def prepare_block3():
                dve.wait_ge(s_set, 12)
                dve.wait_ge(s_k3l, 16 * 12)
                for w, rows_, g in ((kv_w, P, 32), (bias_raw, C, 16)):
                    v = w[:].rearrange("p (g e) -> p g e", e=HD)
                    m = centre[0:rows_, 0:g]
                    link(nc.vector.tensor_reduce(m, v, axis=AX.X, op=ALU.add))
                    link(nc.vector.tensor_scalar(m, m, 1.0 / HD, None, ALU.mult))
                    link(nc.vector.tensor_tensor(v, v, m.unsqueeze(2).to_broadcast([rows_, g, HD]), ALU.subtract))
                link(nc.vector.tensor_copy(bias_hi[:], bias_raw[:]))
                for r in range(4):
                    nc.vector.tensor_copy(bias_rows[0:1, r, :], bias_raw[0:1, :])
                    nc.vector.tensor_tensor(bias_rows[32:33, r, :], bias_raw[32:33, :], bias_hi[32:33, :].bitcast(F32), ALU.subtract)
                rows4 = ln_rows[:].rearrange("p (v a) n -> p v a n", a=2)
                for v in range(2):
                    nc.vector.tensor_tensor(uv[:, v, :], rows4[:, v, 0, :], ln_pat[:, 0, :], ALU.mult)
                    ins = nc.vector.tensor_tensor(uv_t[:, v, :], rows4[:, v, 1, :], ln_pat[:, 1, :], ALU.mult)
                link(ins)
                link(nc.vector.tensor_tensor(uv[:], uv[:], uv_t[:], ALU.add))

            for j in range(CHUNKS):
                if j == CHUNKS // 2:
                    prepare_block3()
                dve.wait_ge(s_x[j], 16)
                for b in range(B):
                    ins = nc.vector.bn_stats(stats[:, b, j, :], state[:, j * CR:(j + 1) * CR, b, :])
            link(ins)
            dve.wait_ge(s_const, 16 * 9)
            link(nc.vector.tensor_scalar(sweep_nbias[:], sweep_bias[:], -1.0, None, ALU.mult))
            group_norm()
            link(nc.vector.tensor_tensor(gn_t[:, 2, :], gn_var[:], gn_a[:], ALU.mult))
            to_pe(nc.vector.tensor_tensor(gn_t[:, 2, :], gn_t[:, 2, :], gn_a[:], ALU.mult))
            rsqrt(gn_t[:, 3, :], bank[7][:, 0:B])
            gw, gb, b1, b2 = (vecs[:, i:i + 1] for i in range(4))
            link(nc.vector.tensor_scalar(gn_t[:, 3, :], gn_t[:, 3, :], gw, None, ALU.mult))
            link(nc.vector.tensor_tensor(aff[:, 0, :], gn_a[:], gn_t[:, 3, :], ALU.mult))
            link(nc.vector.tensor_tensor(aff[:, 1, :], gn_c[:], gn_t[:, 3, :], ALU.mult))
            to_pe(nc.vector.tensor_scalar(aff[:, 1, :], aff[:, 1, :], gb, None, ALU.add))
            link(nc.vector.tensor_scalar(ffn1_b[:], bank[7][:, 0:B], b1, None, ALU.add))
            for b in range(B):
                link(nc.vector.tensor_scalar(ffn1_s[:, b, :], ffn1_w[:], aff[:, 0, b:b + 1], None, ALU.mult))
            link(nc.vector.tensor_scalar(a1[:], gn_a[:], 1.0, None, ALU.add))
            nc.vector.tensor_scalar(cb[:], gn_c[:], b2, None, ALU.add).then_inc(s_coef, 1)

            def ffn(layer, with_stats):
                base = B * CHUNKS * layer
                sbase = B * CHUNKS + 2 * CHUNKS if layer else 0
                with dve.Fori(0, CHUNKS) as j:
                    for b in range(B):
                        dve.wait_ge(s_xs, j * B + (base + b + 1))
                        dve.wait_ge(s_dn, j * B + (base + b + 1))
                        xs = state[:, bass.ts(j, CR), b, :]
                        nc.vector.tensor_tensor(xs, bank[2 + b % 2].rearrange("p (r w) -> p r w", r=CR), xs,
                                                ALU.add).then_inc(s_sum, 1)
                        if with_stats:
                            dve.wait_ge(s_sum, j * B + (sbase + b + 1))
                            nc.vector.bn_stats(stats[:, b, j, :], xs).then_inc(s_dve, 1)
                if with_stats:
                    chain[0] += CHUNKS * B
                    dve.wait_ge(s_dve, chain[0])

            ffn(0, True)
            if STOP < 1:
                return

            def sweep(n):
                layer, along, rev = sweeps[n]
                h0, r0, n0 = hbase(n), row_count(n), STEPS * n
                turning = n % 4 == 1
                nb = sweep_nbias[:, n:n + 1]

                if not rev:
                    dve.wait_ge(s_row, r0 + 1)
                    for c in range(2):
                        new = state[:, 0, 2 * c:2 * c + 2, :] if along == "H" else biased_row[:, 0, 2 * c:2 * c + 2, :]
                        nc.vector.tensor_copy(x_row[c][0][:, :, 2:2 + HALF], new).then_inc(s_h[c], 1)

                def step(i, k, c, ring=0):
                    par = slot(n, k)
                    dve.wait_ge(s_conv[c], i * 2 + (n0 + k))
                    if c == 0:
                        dve.wait_ge(s_row, i * 2 + (r0 + k + (0 if n % 4 == 3 else 1)))
                    ps = bank[2 * c + par][:, 0:2 * HALF].rearrange("p (b w) -> p b w", b=2)
                    br = biased_row[:, k, 2 * c:2 * c + 2, :]
                    new = turn_ring[:, ring, 1 - k, 2 * c:2 * c + 2, :] if turning else cells(n, c, i, k)
                    nc.vector.scalar_tensor_tensor(x_row[c][par][:, :, 2:2 + HALF], ps, nb, br,
                                                   ALU.max, ALU.add).then_inc(s_h[c], 1)
                    nc.vector.scalar_tensor_tensor(new, ps, nb, br, ALU.max, ALU.add).then_inc(s_new[c], 1)
                for c in range(2):
                    step(0, 1, c)
                if turning:
                    def pair(i, k, left):
                        if left is not None:
                            dve.wait_ge(s_turn[k], left)
                        for r in range(2):
                            for c in range(2):
                                step(i, r, c, k)
                    gone = 64 * (PAIRS // 2) * layer
                    pair(1, 1, gone if layer else None)
                    with dve.Fori(1, PAIRS // 2) as m:
                        for k in range(2):
                            pair(m * 2 + k, k, m * 64 + gone)
                else:
                    with dve.Fori(1, PAIRS) as i:
                        for k in range(2):
                            for c in range(2):
                                step(i, k, c)

            def add_residual(layer):
                for c in range(2):
                    dve.wait_ge(s_new[c], STEPS * 4 * (layer + 1))
                for j in range(CHUNKS):
                    dve.wait_ge(s_rld[j % RING], 16 * (CHUNKS // RING * layer + j // RING + 1))
                    rows = state[:, j * CR:(j + 1) * CR, :, :]
                    nc.vector.tensor_tensor(rows, rows, res[:, j % RING, :, :].rearrange("p r (b w) -> p r b w", b=B),
                                            ALU.add).then_inc(s_add, 1)
                    dve.wait_ge(s_add, CHUNKS * layer + j + 1)
                    for b in range(B):
                        ins = nc.vector.bn_stats(stats[:, b, j, :], state[:, j * CR:(j + 1) * CR, b, :])
                    ins.then_inc(s_sum, 1)
                dve.wait_ge(s_sum, B * CHUNKS + CHUNKS * (layer + 1))

            for layer in range(2 if STOP >= 2 else 1):
                group_norm()
                nc.vector.tensor_scalar(aff[:, 0, :], gn_c[:], sweep_bias[:, 4 * layer:4 * layer + 1], None,
                                        ALU.add).then_inc(s_coef, 1)
                for n in range(4 * layer, 4 * layer + 4):
                    sweep(n)
                if STOP < 2:
                    return
                add_residual(layer)

            if STOP < 3:
                return
            group_norm()
            link(nc.vector.tensor_scalar(a1[:], gn_a[:], 1.0, None, ALU.add))
            nc.vector.tensor_scalar(cb[:], gn_c[:], vecs[:, 5:6], None, ALU.add).then_inc(s_coef, 1)

            def kv_sum(b, j, started):
                k, n = b % 2, j * B + b
                dve.wait_ge(s_sqr, n + 1)
                if started or b >= 2:
                    dve.wait_ge(s_sd, n - 1)
                nc.vector.tensor_reduce(ssum[:, k, :], sq[:, k, :].rearrange("p (g e) -> p g e", e=HD),
                                        axis=AX.X, op=ALU.add).then_inc(s_ss, 1)

            def kv_scale(k, n, started, m):
                dve.wait_ge(s_sd, n + 1)
                if started:
                    dve.wait_ge(s_tl, n - 1)
                    dve.wait_ge(s_gr, n - 1)
                nc.vector.tensor_scalar(dev[:, k, :], sdev[:, k, :], EPS, None, ALU.add).then_inc(s_dv, 1)
                dve.wait_ge(s_dv, m + 1)
                nc.vector.reciprocal(rinv[:, k, :], dev[:, k, :]).then_inc(s_ri, 1)
                dve.wait_ge(s_ri, n + 1)
                r = rinv[:, k, :].rearrange("p (g v h) -> p g v h", v=2, h=HEADS)
                nc.vector.tensor_tensor(rkv[:, k, :].rearrange("p (g h) -> p g h", h=HEADS), r[:, :, 0, :], r[:, :, 1, :],
                                        ALU.mult).then_inc(s_dv, 1)
                dve.wait_ge(s_dv, m + 2)
                src = pair[k][:].rearrange("p (g v h e) -> p g v h e", v=2, h=HEADS, e=HD)[:, :, 1, :, 0:HD - 1]
                dst = gram_v[:, k, :].rearrange("p (g h e) -> p g h e", h=HEADS, e=HD)[:, :, :, 0:HD - 1]
                by = rkv[:, k, :].rearrange("p (g h) -> p g h", h=HEADS).unsqueeze(3).to_broadcast([P, 8, HEADS, HD - 1])
                nc.vector.tensor_tensor(dst, src, by, ALU.mult).then_inc(s_vs, 1)

            def kv_step(j, b, started):
                kv_sum(b, j, started)
                if started or b >= 1:
                    kv_scale((b + 1) % 2, j * B + (b - 1), started or b >= 3, j * (2 * B) + 2 * (b - 1))

            for b in range(B):
                kv_step(0, b, False)
            with dve.Fori(1, CHUNKS) as j:
                for b in range(B):
                    kv_step(j, b, True)
            kv_scale(1, B * CHUNKS - 1, True, 2 * (B * CHUNKS - 1))

            dve.wait_ge(s_gr, B * CHUNKS)
            for b in range(B):
                ins = nc.vector.tensor_tensor(gram_sb[:, b, :], bank[4 + b][:, 0:P], gmask[:], ALU.mult)
            to_pe(ins)
            to_pe(nc.vector.tensor_copy(t1_sb, bank[0][:, 0:B * C]))
            to_pe(nc.vector.tensor_scalar(kvt_sb[0:C, :, :], bank[1][0:C, 0:B * C].rearrange("p (b n) -> p b n", b=B),
                                          1.0 / N_PIX, None, ALU.mult))
            for r in range(2):
                nc.vector.tensor_copy(ht_dup[0:C, :, r, :], bank[2][0:C, 0:B * C].rearrange("p (b n) -> p b n", b=B))
            to_pe(nc.vector.tensor_copy(ht_sb[0:C, :], bank[2][0:C, 0:B * C]))
            link(nc.vector.tensor_tensor(gt_sb, bank[3][:, 0:B * C].rearrange("p (b n) -> p b n", b=B),
                                         o1_t[:].unsqueeze(1).to_broadcast([P, B, C]), ALU.add))
            for r in range(2):
                ins = nc.vector.tensor_copy(gt_dup[0:C, :, r, :], gt_sb[0:C, :, :])
            to_pe(ins)
            nc.vector.tensor_scalar(ffn1_b[:], bank[0][:, 0:B], vecs[:, 4:5], None, ALU.add)
            for b in range(B):
                for q in range(2):
                    blk = slice(q * C, (q + 1) * C)
                    ins = nc.vector.tensor_scalar(ffn1_s[blk, b, blk], gt_sb[blk, b, :], gn_a[blk, b:b + 1], None, ALU.mult)
            ins.then_inc(s_coef, 1)
            ffn(1, False)


def kernel(**inputs):
    import concourse.bacc as _bacc
    from concourse.bass_utils import run_bass_kernel_spmd as _run
    f = {k: np.ascontiguousarray(v) for k, v in inputs.items()}
    B, C, H, W = f["x"].shape
    arrays = {}
    arrays["x"] = f["x"].reshape(B, C, H, W // 2, 2).transpose(4, 1, 2, 0, 3).reshape(2 * C, H, B * W // 2)
    l1 = [f[f"L1_conv_w_{d}"].transpose(1, 2, 0) for d in "durl"]
    l2 = [f[f"L2_conv_kernel_{d}"][:, 0].transpose(2, 1, 0) for d in ("td", "dt", "lr", "rl")]
    arrays["taps"] = np.stack(l1 + l2)
    zero = np.zeros((C,), np.float32)
    arrays["sbias"] = np.stack([np.tile(f[f"L1_conv_b_{d}"], 2) for d in "durl"] + [np.tile(zero, 2)] * 4, axis=1)
    arrays["w1t"] = f["L0_conv_w1"].T
    arrays["w2t"] = f["L0_conv_w2"].T
    arrays["o2t"] = f["L3_conv_o2_w"].T
    arrays["vecs"] = np.stack([np.tile(f[n], 2) for n in ("L0_conv_gn_w", "L0_conv_gn_b", "L0_conv_b1", "L0_conv_b2",
                                                          "L3_conv_o1_b", "L3_conv_o2_b")], axis=1)
    qkv_w, qkv_b = f["L3_conv_qkv_w"].reshape(8, 3, 8, C), f["L3_conv_qkv_b"].reshape(8, 3, 8)
    arrays["wq"] = qkv_w[:, 0].reshape(C, C)
    arrays["bq"] = qkv_b[:, 0].reshape(C, 1)
    arrays["kvt"] = qkv_w[:, 1:].transpose(1, 0, 2, 3).reshape(2 * C, C).T
    arrays["kvb"] = qkv_b[:, 1:].transpose(1, 0, 2).reshape(1, 2 * C)
    arrays["o1t"] = f["L3_conv_o1_w"].T
    ln = np.stack([f[f"L3_conv_{n}"].reshape(C) for n in ("kln_w", "kln_b", "vln_w", "vln_b")])
    arrays["ln_rows"] = np.broadcast_to(ln, (2 * C, 4, C))
    ch = np.arange(2 * C) % C
    e, i, same = ch[:, None] % 8, ch[None, :C] % 8, ch[:, None] // 8 == ch[None, :C] // 8
    weight = same & (e < 7) & (e == i)
    arrays["ln_pat"] = np.stack([weight * 1.0 - (same & (e < 7) & (i == 7)), same & (e == 7)], axis=1).astype(np.float32)
    arrays["gmask"] = (np.arange(2 * C)[:, None] // 8 == np.arange(2 * C)[None, :] // 8).astype(np.float32)
    arrays["gmats"] = np.stack([(ch[:, None] // g == ch[None, :] // g) / (2.0 * g) for g in (2, 8)]).astype(np.float32)
    arrays = {f"{k}_in": np.ascontiguousarray(v) for k, v in arrays.items()}

    nc = _bacc.Bacc("TRN2", target_bir_lowering=False, num_devices=1)
    D = {k[:-3]: nc.dram_tensor(k, v.shape, mybir.dt.from_np(v.dtype), kind="ExternalInput").ap() for k, v in arrays.items()}
    D["resid"] = nc.dram_tensor("resid", (H // 2, 2 * C, 2, B * W // 2), mybir.dt.float32).ap()
    out = nc.dram_tensor("out_y", (2 * C, H * B * W // 2), mybir.dt.float32, kind="ExternalOutput").ap()
    build_program(nc, D, out, None)
    r = _run(nc, [arrays], core_ids=[0])
    y = r.results[0]["out_y"].reshape(2, C, H // 2, 2, B, W // 2)
    return np.ascontiguousarray(y.transpose(4, 1, 2, 0, 5, 3)).reshape(B, C, H, W)
```

```python
import numpy as np
import concourse.bass as bass
from concourse import mybir
from contextlib import ExitStack


def build_program(nc, D, out, debug):
    F32, F32R = mybir.dt.float32, mybir.dt.float32r
    ALU, ACT, AX = mybir.AluOpType, mybir.ActivationFunctionType, mybir.AxisListType
    B, C, H, W = 4, 64, 128, 128
    P = 2 * C
    HALF = W // 2
    ROW = B * HALF
    PAIRS = H // 2
    TAPS2 = 5
    PADDED = HALF + 4
    CR = 8
    CHUNKS = H // CR
    NT = CR * HALF
    RING = 4
    LAG = 3
    EPS = 1e-5
    HEADS, HD = 8, 8
    GROUPS = 8 * 2 * HEADS
    HQ = 2 * HEADS
    N_PIX = H * W

    sweeps = []
    for layer in (0, 1):
        sweeps += [(layer, "H", False), (layer, "H", True), (layer, "W", False), (layer, "W", True)]
    NS = len(sweeps)

    ctx = ExitStack()
    with ctx:
        def sb(name, shape, dt=F32):
            return ctx.enter_context(nc.sbuf_tensor(name, shape, dt))

        def sem(name):
            return ctx.enter_context(nc.semaphore(name))

        state = sb("state", [P, H, B, HALF])
        state_b = state[:].rearrange("p (hp s) b w -> p hp s b w", s=2)
        res = sb("res", [P, RING, CR, ROW])
        x_row = [[sb(f"x_row{c}{k}", [P, 2, PADDED]) for k in range(2)] for c in range(2)]
        biased_row = sb("biased_row", [P, 2, B, HALF])
        turn_ring = sb("turn_ring", [P, 2, 2, B, HALF])
        w_taps = sb("w_taps", [P, 2, TAPS2, P])
        sweep_bias = sb("sweep_bias", [P, NS])
        sweep_nbias = sb("sweep_nbias", [P, NS])
        gmats = sb("gmats", [P, 2, P])
        vecs = sb("vecs", [P, 6])
        stats = sb("stats", [P, B, CHUNKS, 6])
        sums = sb("sums", [P, 2, B, CHUNKS])
        minus_shift = sb("minus_shift", [P, B])
        mv = sb("mv", [P, B, 2])
        gn_mean = sb("gn_mean", [P, B])
        gn_var = sb("gn_var", [P, B])
        gn_a = sb("gn_a", [P, B])
        gn_c = sb("gn_c", [P, B])
        gn_t = sb("gn_t", [P, 4, B])
        a1 = sb("a1", [P, B])
        cb = sb("cb", [P, B])
        aff = sb("aff", [P, 2, B])
        eps_t = sb("eps_t", [P, 1])
        ffn1_w = sb("ffn1_w", [P, P])
        ffn2_w = sb("ffn2_w", [P, 2, P])
        ffn1_s = sb("ffn1_s", [P, B, P])
        ffn1_b = sb("ffn1_b", [P, B])
        hid = sb("hid", [P, 2, NT])
        ring = [0, res[:].rearrange("p a r c -> p (a r c)")]

        def in_ring(n):
            ring[0] += n
            assert ring[0] <= RING * CR * ROW
            return ring[1][:, ring[0] - n:ring[0]]

        def slots(ap):
            return ap.rearrange("p (k n) -> p k n", k=2)

        y_st = slots(in_ring(2 * NT))
        sq = slots(in_ring(4 * NT))
        gram_kv = in_ring(4 * 2 * NT).rearrange("p (k g v h e) -> p k g v h e", k=4, v=2, h=HQ, e=HD)
        ssum = slots(in_ring(2 * GROUPS))
        sdev = slots(in_ring(2 * GROUPS))
        dev = slots(in_ring(2 * GROUPS))
        dprod = slots(in_ring(GROUPS))
        rkv = slots(in_ring(GROUPS))
        gram_sb = sq[:, 0, 0:4 * P].rearrange("p (b n) -> p b n", b=B)
        t1_sb = sq[:, 0, 4 * P:4 * P + B * C]
        kvt_sb = sq[:, 0, 4 * P + B * C:4 * P + 2 * B * C].rearrange("p (b n) -> p b n", b=B)
        ht_sb = sq[:, 1, 0:B * C]
        gt_sb = sq[:, 1, B * C:2 * B * C].rearrange("p (b n) -> p b n", b=B)
        ht_dup = sq[:, 1, 2 * B * C:4 * B * C].rearrange("p (b r n) -> p b r n", b=B, r=2)
        gt_dup = y_st[:, 0, :].rearrange("p (b r n) -> p b r n", b=B, r=2)
        kv_w = sb("kv_w", [P, 2 * P])
        bias_raw = sb("bias_raw", [C, P])
        bias_hi = sb("bias_hi", [C, P], F32R)
        bias_rows = sb("bias_rows", [P, 2, 2, 2, C], F32R)
        ones = sb("ones", [P, P], F32R)
        centre = sb("centre", [P, 32])
        ln_rows = sb("ln_rows", [P, 4, C])
        ln_pat = sb("ln_pat", [P, 2, C])
        uv = sb("uv", [P, 2, C])
        uv_t = sb("uv_t", [P, 2, C])
        gmask = sb("gmask", [P, P])
        wq_dup = sb("wq_dup", [C, 2, C])
        o1_t = sb("o1_t", [P, C])
        bq = sb("bq", [C, 1])

        BANK = 512
        pair = [ctx.enter_context(nc.psum_tensor(f"banks{2 * i}_{2 * i + 1}", [P, 2 * BANK], F32)) for i in range(4)]
        bank = [pair[i // 2][:, (i % 2) * BANK:(i % 2 + 1) * BANK] for i in range(8)]

        resid = D["resid"]

        s_x = [sem(f"s_x{j}") for j in range(CHUNKS)]
        s_const = sem("s_const")
        s_set = sem("s_set")
        s_gp = sem("s_gp")
        s_gq = sem("s_gq")
        s_sq = sem("s_sq")
        s_rt = sem("s_rt")
        s_dve = sem("s_dve")
        s_coef = sem("s_coef")
        s_up = sem("s_up")
        s_act = sem("s_act")
        s_xs = sem("s_xs")
        s_dn = sem("s_dn")
        s_sum = sem("s_sum")
        s_h = [sem(f"s_h{c}") for c in range(2)]
        s_new = [sem(f"s_new{c}") for c in range(2)]
        s_conv = [sem(f"s_conv{c}") for c in range(2)]
        s_row = sem("s_row")
        s_w = [sem(f"s_w{k}") for k in range(2)]
        s_turn = [sem(f"s_turn{k}") for k in range(2)]
        s_rst = sem("s_rst")
        s_rst1 = [sem(f"s_rst1_{j}") for j in range(CHUNKS)]
        s_rld = [sem(f"s_rld{k}") for k in range(RING)]
        s_add = sem("s_add")
        s_shift = sem("s_shift")
        s_sqs = sem("s_sqs")
        s_cross = [sem(f"s_cross{j}") for j in range(CHUNKS)]
        s_out = sem("s_out")
        s_y = sem("s_y")
        s_kv = sem("s_kv")
        s_sqr = sem("s_sqr")
        s_kc = sem("s_kc")
        s_ss = sem("s_ss")
        s_sd = sem("s_sd")
        s_dv = sem("s_dv")
        s_ri = sem("s_ri")
        s_vs = sem("s_vs")
        s_tl = sem("s_tl")
        s_gr = sem("s_gr")
        s_k3 = sem("s_k3")
        s_k3l = sem("s_k3l")

        block = ctx.enter_context(nc.Block())

        STEPS = H - 1

        def hbase(n):
            return sum(STEPS + (0 if rev else 1) for _, _, rev in sweeps[:n])

        def row_count(n):
            return sum(STEPS + (0 if (m % 4 == 3) else 1) for m in range(n))

        def row_of(rev, i, k):
            return (H - 1 - k) - 2 * i if rev else 2 * i + k

        def cells(n, c, i, k):
            _, along, rev = sweeps[n]
            r = row_of(rev, i, k)
            if along == "H":
                return state[:, r, 2 * c:2 * c + 2, :]
            s = (1 - k) if rev else k
            wp = (HALF - 1) - i if rev else i
            return state_b[:, :, s, 2 * c:2 * c + 2, wp].rearrange("p h b -> p b h")

        def slot(n, k):
            return (k + 1) % 2 if sweeps[n][2] else k

        @block.sync
        def _(sp):
            for j in range(CHUNKS):
                sp.dma_start(state[:, j * CR:(j + 1) * CR, :, :], D["x"][:, j * CR:(j + 1) * CR, :]
                             .rearrange("p r (b w) -> p r b w", b=B)).then_inc(s_x[j], 16)

            def store_residual_a(j):
                for q in range(2):
                    for r in range(2):
                        src = state[q * C:(q + 1) * C, :, :, :].rearrange(
                            "c (j hp r) b w -> c j hp r (b w)", r=2, hp=CR // 2)[:, j, :, r, :]
                        dst = resid.rearrange("(j hp) (r c) s n -> j r c s hp n", hp=CR // 2, r=2)[j, r, :, q, :, :]
                        sp.dma_start(dst, src).then_inc(s_rst, 16)

            with sp.Fori(0, CHUNKS) as j:
                sp.wait_ge(s_sum, j * B + B)
                store_residual_a(j)

            for layer in (0, 1):
                n = 4 * layer + 1
                sp.wait_ge(s_new[0], STEPS * n + 1)
                sp.wait_ge(s_new[1], STEPS * n + 1)
                sp.wait_ge(s_row, row_count(n) + 2)

                def turn(m, k):
                    hp = m * -2 + (PAIRS - 1 - k)
                    for s in range(2):
                        for q in range(2):
                            sp.dma_start(state_b[q * C:(q + 1) * C, hp, s, :, :],
                                         turn_ring[s * C:(s + 1) * C, k, q, :, :]).then_inc(s_turn[k], 16)
                turn(0, 0)
                sp.wait_ge(s_new[0], STEPS * n + 3)
                sp.wait_ge(s_new[1], STEPS * n + 3)
                turn(0, 1)
                with sp.Fori(1, PAIRS // 2) as m:
                    for k in range(2):
                        sp.wait_ge(s_new[0], m * 4 + (STEPS * n + 2 * k + 1))
                        sp.wait_ge(s_new[1], m * 4 + (STEPS * n + 2 * k + 1))
                        turn(m, k)
                if layer == 0:
                    sp.wait_ge(s_rst, 16 * 4 * CHUNKS)
                else:
                    for j in range(CHUNKS):
                        sp.wait_ge(s_rst1[j], 16)
                for j in range(CHUNKS):
                    if j >= RING:
                        sp.wait_ge(s_add, layer * CHUNKS + j - RING + 1)
                    sp.dma_start(res[:, j % RING, :, :].rearrange("p (hp s) n -> p hp (s n)", s=2),
                                 resid.rearrange("hp p s n -> p hp (s n)")[:, j * CR // 2:(j + 1) * CR // 2, :]
                                 ).then_inc(s_rld[j % RING], 16)
                if layer == 0:
                    def cross(j):
                        sp.wait_ge(s_rst1[j], 16)
                        sp.wait_ge(s_sqs, B * (j + 1))
                        for q in range(2):
                            sp.dma_start(state_b[q * C:(q + 1) * C, j * CR // 2:(j + 1) * CR // 2, 1 - q, :, :],
                                         resid.rearrange("hp (r c) s (b w) -> r c hp s b w", r=2, b=B)
                                         [1 - q, :, j * CR // 2:(j + 1) * CR // 2, q, :, :]).then_inc(s_cross[j], 16)

                    for j in range(CHUNKS):
                        sp.wait_ge(s_add, j + 1)
                        sp.wait_ge(s_rld[j % RING], 16 * (j // RING + 1))
                        sp.dma_start(resid.rearrange("hp p s n -> p hp (s n)")[:, j * CR // 2:(j + 1) * CR // 2, :],
                                     state[:, j * CR:(j + 1) * CR, :, :].rearrange("p (hp s) b w -> p hp (s b w)", s=2)
                                     ).then_inc(s_rst1[j], 16)
                        if j >= 2:
                            cross(j - 2)
                    cross(CHUNKS - 2)
                    cross(CHUNKS - 1)
            with sp.Fori(0, CHUNKS) as j:
                sp.wait_ge(s_sum, j * B + (B * CHUNKS + B))
                sp.dma_start(out[:, bass.ts(j, CR * ROW)], state[:].rearrange("p (j r) b w -> p j (r b w)", r=CR)[:, j, :]
                             ).then_inc(s_out, 16)
            sp.wait_ge(s_out, 16 * CHUNKS)

        @block.gpsimd
        def _(pool):
            nc.gpsimd.memset(eps_t[:], EPS).then_inc(s_set, 1)
            nc.gpsimd.memset(w_taps[:], 0.0).then_inc(s_set, 1)
            nc.gpsimd.memset(ffn1_w[:], 0.0).then_inc(s_set, 1)
            nc.gpsimd.memset(ffn2_w[:], 0.0).then_inc(s_set, 1)
            for c in range(2):
                for k in range(2):
                    nc.gpsimd.memset(x_row[c][k][:], 0.0).then_inc(s_set, 1)
            nc.gpsimd.memset(kv_w[:], 0.0).then_inc(s_set, 1)
            nc.gpsimd.memset(bias_raw[:], 0.0).then_inc(s_set, 1)
            nc.gpsimd.memset(bias_rows[:].bitcast(F32), 0.0).then_inc(s_set, 1)
            nc.gpsimd.memset(ones[:].bitcast(F32), 1.0).then_inc(s_set, 1)

            def tails(b, n, started):
                k = b % 2
                pool.wait_ge(s_kc, n + 1)
                pool.wait_ge(s_ri, n + 1)
                d = dev[:, k, :].rearrange("p (g v h) -> p g v h", v=2, h=HQ)
                nc.gpsimd.tensor_tensor(gram_kv[:, b, :, 0, :, HD - 1], d[:, :, 0, :],
                                        ones[:, 0:4 * HQ].bitcast(F32).rearrange("p (g h) -> p g h", h=HQ), ALU.mult)
                nc.gpsimd.tensor_tensor(gram_kv[:, b, :, 1, :, HD - 1], d[:, :, 1, :],
                                        rkv[:, k, :].rearrange("p (g h) -> p g h", h=HQ), ALU.mult).then_inc(s_tl, 1)

            for b in range(B):
                tails(b, b, b >= 2)
            with pool.Fori(1, CHUNKS) as j:
                for b in range(B):
                    tails(b, j * B + b, True)

        @block.scalar
        def _(act):
            act.wait_ge(s_set, 12)
            for dst, src in ((gmats[:], D["gmats"].rearrange("g p q -> p g q")), (vecs[:], D["vecs"]), (sweep_bias[:], D["sbias"])):
                act.dma_start(dst, src).then_inc(s_const, 16)
            for q in range(2):
                blk = slice(q * C, (q + 1) * C)
                act.dma_start(ffn1_w[blk, blk], D["w1t"]).then_inc(s_const, 16)
                act.dma_start(ffn2_w[blk, 0, blk], D["w2t"]).then_inc(s_const, 16)
                act.dma_start(ffn2_w[blk, 1, blk], D["o2t"]).then_inc(s_const, 16)

                act.dma_start(kv_w[:].rearrange("p (v q n) -> p v q n", v=2, q=2)[blk, :, q, :],
                              D["kvt"].rearrange("c (v n) -> c v n", v=2)).then_inc(s_k3l, 16)
                act.dma_start(bias_raw[32 * q:32 * q + 1, :], D["kvb"]).then_inc(s_k3l, 16)
                act.dma_start(wq_dup[:, q, :], D["wq"]).then_inc(s_k3l, 16)
                act.dma_start(o1_t[blk, :], D["o1t"]).then_inc(s_k3l, 16)
            for dst, name in ((bq[:], "bq"), (ln_rows[:], "ln_rows"), (ln_pat[:], "ln_pat"), (gmask[:], "gmask")):
                act.dma_start(dst, D[name]).then_inc(s_k3l, 16)

            def load_taps(n):
                if n >= 2:
                    act.wait_ge(s_conv[1], STEPS * (n - 1))
                for q in range(2):
                    for r in range(2):
                        taps = [(s, 2 * s + q - r) for s in range(TAPS2) if 0 <= 2 * s + q - r <= 8]
                        s0, t0, cnt = taps[0][0], taps[0][1], len(taps)
                        act.dma_start(w_taps[q * C:(q + 1) * C, n % 2, s0:s0 + cnt, r * C:(r + 1) * C],
                                      D["taps"][n, :, t0:t0 + 2 * cnt - 1:2, :]).then_inc(s_w[n % 2], 16)

            load_taps(0)

            def root(k):
                act.wait_ge(s_sq, k)
                nc.scalar.activation(gn_t[:, 1, :], gn_t[:, 0, :], ACT.Sqrt, bias=eps_t[:]).then_inc(s_rt, 1)

            root(1)
            root(2)

            def ffn(layer, func):
                base = B * CHUNKS * layer
                act.wait_ge(s_coef, 5 if layer else 1)
                def tile(j, b):
                    t = j * B + (b + base)
                    act.wait_ge(s_up, t + 1)
                    nc.scalar.activation(hid[:, b % 2, :], bank[b % 2], func, bias=ffn1_b[:, b:b + 1]).then_inc(s_act, 1)
                    xs = state[:, bass.ts(j, CR), b, :]
                    nc.scalar.activation(xs, xs, ACT.Identity, scale=a1[:, b:b + 1], bias=cb[:, b:b + 1]).then_inc(s_xs, 1)
                with act.Fori(0, CHUNKS) as j:
                    for b in range(B):
                        tile(j, b)

            ffn(0, ACT.Relu)

            def rows(n):
                layer, along, rev = sweeps[n]
                first, start = n % 4 == 0, row_count(n)
                if n + 1 < NS:
                    load_taps(n + 1)
                if first:
                    root(3 + layer)
                    act.wait_ge(s_coef, 2 + layer)
                    if layer == 0:
                        act.wait_ge(s_rst, 16 * 4 * CHUNKS)
                    else:
                        act.wait_ge(s_cross[0], 32)
                if n % 4 == 2:
                    for k in range(2):
                        act.wait_ge(s_turn[k], 64 * (PAIRS // 2) * (layer + 1))
                elif n % 4 != 0:
                    act.wait_ge(s_new[0], STEPS * n)
                    act.wait_ge(s_new[1], STEPS * n)

                def row(i, k):
                    if first:
                        for b in range(B):
                            src = state[:, row_of(rev, i, k), b, :]
                            last = nc.scalar.activation(biased_row[:, k, b, :], src, ACT.Identity,
                                                        scale=gn_a[:, b:b + 1], bias=aff[:, 0, b:b + 1])
                        last.then_inc(s_row, 1)
                        return
                    if along == "H":
                        src = state[:, row_of(rev, i, k), :, :]
                    else:
                        s = (1 - k) if rev else k
                        src = state_b[:, :, s, :, (HALF - 1) - i if rev else i].rearrange("p h b -> p b h")
                    nc.scalar.activation(biased_row[:, k, :, :], src, ACT.Identity,
                                         bias=sweep_bias[:, n:n + 1]).then_inc(s_row, 1)

                if first:
                    for b in range(B):
                        xs = state[:, 0, b, :]
                        last = nc.scalar.activation(xs, xs, ACT.Identity, scale=gn_a[:, b:b + 1], bias=gn_c[:, b:b + 1])
                    last.then_inc(s_row, 1)
                elif n % 4 == 1:
                    nc.scalar.activation(turn_ring[:, 0, 1, :, :], state[:, H - 1, :, :], ACT.Copy).then_inc(s_row, 1)
                elif n % 4 == 2:
                    nc.scalar.activation(biased_row[:, 0, :, :], state_b[:, :, 0, :, 0].rearrange("p h b -> p b h"),
                                         ACT.Copy).then_inc(s_row, 1)
                row(0, 1)

                def next_row(i, k):
                    for c in range(2):
                        act.wait_ge(s_h[c], i * 2 + (hbase(n) + k - 2 + (0 if rev else 1)))
                        if not isinstance(i, int) or STEPS * n + k:
                            act.wait_ge(s_new[c], i * 2 + (STEPS * n + k - 2))
                    row(i, k)

                if n == 0:
                    next_row(1, 0)
                    next_row(1, 1)
                if n == 4:
                    for j in range(CHUNKS):
                        if j:
                            act.wait_ge(s_cross[j], 32)
                        with act.Fori(max(j * CR // 2, 1), (j + 1) * CR // 2) as i:
                            for k in range(2):
                                next_row(i, k)
                else:
                    with act.Fori(2 if n == 0 else 1, PAIRS) as i:
                        for k in range(2):
                            next_row(i, k)

            def sums_of_squares(layer):
                act.wait_ge(s_shift, layer + 1)
                for j in range(CHUNKS):
                    act.wait_ge(s_add, layer * CHUNKS + j + 1)
                    for b in range(B):
                        if j:
                            act.wait_ge(s_sqs, B * (layer * CHUNKS + j - 1) + b + 1)
                        nc.scalar.activation(bank[4 + b].rearrange("p (r w) -> p r w", r=CR),
                                             state[:, j * CR:(j + 1) * CR, b, :], ACT.Square,
                                             bias=minus_shift[:, b:b + 1], accum_out=sums[:, 1, b, j:j + 1]).then_inc(s_sqs, 1)

            for n in range(4):
                rows(n)
            sums_of_squares(0)
            for n in range(4, 8):
                rows(n)
            sums_of_squares(1)
            root(5)
            act.wait_ge(s_coef, 4)

            def kv_root(k, n):
                act.wait_ge(s_ss, n + 1)
                nc.scalar.activation(sdev[:, k, :], ssum[:, k, :], ACT.Sqrt, scale=1.0 / (HD - 1)).then_inc(s_sd, 1)

            def kv_square(b, n, started):
                k = b % 2
                act.wait_ge(s_kv, n + 1)
                if started or b >= 2:
                    act.wait_ge(s_ss, n - 1)
                nc.scalar.activation(sq[:, k, :], pair[k][:], ACT.Square).then_inc(s_sqr, 1)
                if started:
                    act.wait_ge(s_gr, n - 3)
                nc.scalar.activation(gram_kv[:, b, :, :, :, :].rearrange("p g v h e -> p (g v h e)"), pair[k][:],
                                     ACT.Copy).then_inc(s_kc, 1)

            def kv_stage(j, b, started, after_first=False):
                n = j * B + b
                if started or b >= 2:
                    act.wait_ge(s_kv, n - 1)
                nc.scalar.activation(y_st[:, b % 2, :].rearrange("p (r w) -> p r w", r=CR), state[:, bass.ts(j, CR), b, :],
                                     ACT.Identity, scale=gn_a[:, b:b + 1], bias=gn_c[:, b:b + 1]).then_inc(s_y, 1)
                if started or b >= 2:
                    kv_root(b % 2, n - 2)
                if started or b >= 1:
                    kv_square((b - 1) % B, n - 1, started and b >= 1 or after_first)

            for m in range(2 * B):
                kv_stage(m // B, m % B, m >= B)
            with act.Fori(2, CHUNKS) as j:
                for b in range(B):
                    kv_stage(j, b, True, True)
            n = B * CHUNKS
            kv_root(0, n - 2)
            kv_square(B - 1, n - 1, True)
            kv_root(1, n - 1)
            ffn(1, ACT.Gelu)

        @block.tensor
        def _(pe):
            steps = [0]

            def stat_product(g, cols):
                steps[0] += 1
                pe.wait_ge(s_gp, steps[0])
                nc.tensor.matmul(bank[7][:, 0:cols.shape[-1]], gmats[:, g, :], cols, start=True, stop=True).then_inc(s_gq, 1)

            pe.wait_ge(s_const, 16 * 9)
            stat_product(0, gn_t[:, 2, :])
            stat_product(0, gn_t[:, 3, :])
            stat_product(1, gn_t[:, 2, :])
            steps[0] += 1
            pe.wait_ge(s_gp, steps[0])
            nc.tensor.matmul(bank[7][:, 0:B], ffn1_w[:], aff[:, 1, :], start=True, stop=True).then_inc(s_gq, 1)

            def ffn(layer):
                base = B * CHUNKS * layer
                pe.wait_ge(s_coef, 5 if layer else 1)

                def up(j, b):
                    nc.tensor.matmul(bank[b % 2], ffn1_s[:, b, :], state[:, bass.ts(j, CR), b, :],
                                     start=True, stop=True).then_inc(s_up, 1)

                def down(b):
                    nc.tensor.matmul(bank[2 + b % 2], ffn2_w[:, layer, :], hid[:, b % 2, :],
                                     start=True, stop=True).then_inc(s_dn, 1)

                def second(j, b, start):
                    pe.wait_ge(s_act, j * B + (base + b + 1))
                    if b >= 2 or not start:
                        pe.wait_ge(s_sum, j * B + (base + b - 1))
                    down(b)

                def chunk(j, start):
                    for b in range(B):
                        up(j, b)
                        if b:
                            second(j, b - 1, start)
                    second(j, B - 1, start)
                chunk(0, True)
                with pe.Fori(1, CHUNKS) as j:
                    chunk(j, False)

            ffn(0)

            def conv(n, c, k, hcount):
                par, src = slot(n, k), slot(n, 1 - k)
                out_ps = bank[2 * c + par][:, 0:2 * HALF].rearrange("p (b w) -> p b w", b=2)
                pe.wait_ge(s_h[c], hcount)
                for s in range(TAPS2):
                    last = nc.tensor.matmul(out_ps, w_taps[:, n % 2, s, :], x_row[c][src][:, :, s:s + HALF],
                                            start=s == 0, stop=s == TAPS2 - 1)
                last.then_inc(s_conv[c], 1)

            def sweep(n):
                rev = sweeps[n][2]
                before = hbase(n) + (0 if rev else 1)
                pe.wait_ge(s_w[n % 2], 64 * (n // 2 + 1))
                for c in range(2):
                    conv(n, c, 1, before)
                with pe.Fori(1, PAIRS) as i:
                    for k in range(2):
                        for c in range(2):
                            conv(n, c, k, i * 2 + (before + k - 1))

            for n in range(NS):
                if n % 4 == 0:
                    stat_product(0, gn_t[:, 2, :])
                    stat_product(0, gn_t[:, 3, :])
                sweep(n)
            stat_product(0, gn_t[:, 2, :])
            stat_product(0, gn_t[:, 3, :])

            def kv_products(j, b, started):
                k, n = b % 2, j * B + b
                pe.wait_ge(s_y, n + 1)
                if started or b >= 2:
                    pe.wait_ge(s_kc, n - 1)
                for u in range(2):
                    ps = pair[k][:, u * BANK:(u + 1) * BANK]
                    nc.tensor.matmul(ps, ones[:], bias_rows[:].rearrange("p t v q n -> p (t v q n)"), start=True, stop=False)
                    for t in range(2):
                        col = (2 * u + t) * P
                        last = nc.tensor.matmul(ps[:, t * 2 * P:(t + 1) * 2 * P], y_st[:, k, col:col + P], kv_w[:],
                                                start=False, stop=t == 1)
                last.then_inc(s_kv, 1)

            def gram(b, n):
                pe.wait_ge(s_vs, n + 1)
                pe.wait_ge(s_tl, n + 1)
                for t in range(4):
                    part = gram_kv[:, b, t, :, :, :].rearrange("p v h e -> p v (h e)")
                    last = nc.tensor.matmul(bank[4][:, b * P:(b + 1) * P], part[:, 0, :], part[:, 1, :],
                                            start=isinstance(n, int) and n == 0 and t == 0,
                                            stop=isinstance(n, int) and n >= B * (CHUNKS - 1) and t == 3, skip_group_check=True)
                last.then_inc(s_gr, 1)

            for b in range(B):
                kv_products(0, b, False)
                if b == B - 1:
                    gram(0, 0)
            with pe.Fori(1, CHUNKS) as j:
                for b in range(B):
                    kv_products(j, b, True)
                    gram((b - LAG) % B, j * B + (b - LAG))
            for m in range(B * CHUNKS - LAG, B * CHUNKS):
                gram(m % B, m)

            def operands():
                steps[0] += 1
                pe.wait_ge(s_gp, steps[0])

            operands()
            for b in range(B):
                last = nc.tensor.matmul(bank[0][:, b * C:(b + 1) * C], gram_sb[:, b, :], uv[:, 0, :], start=True, stop=True)
            last.then_inc(s_gq, 1)
            operands()
            nc.tensor.matmul(bank[1][0:C, 0:B * C], uv[:, 1, :], t1_sb, start=True, stop=True).then_inc(s_gq, 1)
            operands()
            for b in range(B):
                last = nc.tensor.matmul(bank[2][0:C, b * C:(b + 1) * C], kvt_sb[0:C, b, :], o1_t[0:C, :], start=True, stop=True)
            last.then_inc(s_gq, 1)
            operands()
            nc.tensor.matmul(bank[3][:, 0:B * C], wq_dup[:].rearrange("p r n -> p (r n)"), ht_sb[0:C, :],
                             start=True, stop=True).then_inc(s_gq, 1)
            operands()
            for b in range(B):
                nc.tensor.matmul(bank[0][:, b:b + 1], gt_dup[0:C, b, :, :].rearrange("p r n -> p (r n)"), gn_c[0:C, b:b + 1],
                                 start=True, stop=False)
                last = nc.tensor.matmul(bank[0][:, b:b + 1], ht_dup[0:C, b, :, :].rearrange("p r n -> p (r n)"), bq[:],
                                        start=False, stop=True)
            last.then_inc(s_gq, 1)
            ffn(1)

        @block.vector
        def _(dve):
            chain = [0]

            def link(ins):
                chain[0] += 1
                ins.then_inc(s_dve, 1)
                dve.wait_ge(s_dve, chain[0])

            gp, gq, rt = [0], [0], [0]

            def to_pe(ins):
                ins.then_inc(s_gp, 1)
                gq[0] += 1
                dve.wait_ge(s_gq, gq[0])

            def rsqrt(dst, var):
                nc.vector.tensor_copy(gn_t[:, 0, :], var).then_inc(s_sq, 1)
                rt[0] += 1
                dve.wait_ge(s_rt, rt[0])
                link(nc.vector.reciprocal(dst, gn_t[:, 1, :]))

            def from_bn_stats():
                for b in range(B):
                    ins = nc.vector.bn_aggr(mv[:, b, :], stats[:, b, :, :].rearrange("p j s -> p (j s)"))
                link(ins)

            def from_sums():
                n = CR * HALF * CHUNKS
                link(nc.vector.tensor_reduce(gn_t[:, 2:4, :], sums[:], axis=AX.X, op=ALU.add))
                link(nc.vector.tensor_scalar(gn_t[:, 2:4, :], gn_t[:, 2:4, :], 1.0 / n, None, ALU.mult))
                nc.vector.tensor_copy(mv[:, :, 0], gn_t[:, 2, :])
                link(nc.vector.tensor_tensor(gn_t[:, 0, :], gn_t[:, 2, :], minus_shift[:], ALU.add))
                link(nc.vector.tensor_tensor(gn_t[:, 0, :], gn_t[:, 0, :], gn_t[:, 0, :], ALU.mult))
                link(nc.vector.tensor_tensor(mv[:, :, 1], gn_t[:, 3, :], gn_t[:, 0, :], ALU.subtract))

            def group_norm():
                to_pe(nc.vector.tensor_copy(gn_t[:, 2, :], mv[:, :, 0]))
                link(nc.vector.tensor_copy(gn_mean[:], bank[7][:, 0:B]))
                link(nc.vector.tensor_tensor(gn_t[:, 0, :], mv[:, :, 0], gn_mean[:], ALU.subtract))
                link(nc.vector.tensor_tensor(gn_t[:, 0, :], gn_t[:, 0, :], gn_t[:, 0, :], ALU.mult))
                to_pe(nc.vector.tensor_tensor(gn_t[:, 3, :], gn_t[:, 0, :], mv[:, :, 1], ALU.add))
                link(nc.vector.tensor_copy(gn_var[:], bank[7][:, 0:B]))
                rsqrt(gn_a[:], gn_var[:])
                link(nc.vector.scalar_tensor_tensor(gn_c[:], gn_mean[:], -1.0, gn_a[:], ALU.mult, ALU.mult))

            def prepare_block3():
                dve.wait_ge(s_set, 12)
                dve.wait_ge(s_k3l, 16 * 12)
                for w, rows_, g in ((kv_w, P, 32), (bias_raw, C, 16)):
                    v = w[:].rearrange("p (g e) -> p g e", e=HD)
                    m = centre[0:rows_, 0:g]
                    link(nc.vector.tensor_reduce(m, v, axis=AX.X, op=ALU.add))
                    link(nc.vector.tensor_scalar(m, m, 1.0 / HD, None, ALU.mult))
                    link(nc.vector.tensor_tensor(v, v, m.unsqueeze(2).to_broadcast([rows_, g, HD]), ALU.subtract))
                link(nc.vector.tensor_copy(bias_hi[:], bias_raw[:]))
                by_kv = bias_raw[:].rearrange("p (v n) -> p v n", v=2)
                hi_kv = bias_hi[:].bitcast(F32).rearrange("p (v n) -> p v n", v=2)
                for t in range(2):
                    for q in range(2):
                        nc.vector.tensor_copy(bias_rows[0:1, t, :, q, :], by_kv[0:1, :, :])
                        nc.vector.tensor_tensor(bias_rows[32:33, t, :, q, :], by_kv[32:33, :, :], hi_kv[32:33, :, :], ALU.subtract)
                rows4 = ln_rows[:].rearrange("p (v a) n -> p v a n", a=2)
                for v in range(2):
                    nc.vector.tensor_tensor(uv[:, v, :], rows4[:, v, 0, :], ln_pat[:, 0, :], ALU.mult)
                    ins = nc.vector.tensor_tensor(uv_t[:, v, :], rows4[:, v, 1, :], ln_pat[:, 1, :], ALU.mult)
                link(ins)
                link(nc.vector.tensor_tensor(uv[:], uv[:], uv_t[:], ALU.add))

            for j in range(CHUNKS):
                if j == CHUNKS - 1:
                    prepare_block3()
                dve.wait_ge(s_x[j], 16)
                for b in range(B):
                    ins = nc.vector.bn_stats(stats[:, b, j, :], state[:, j * CR:(j + 1) * CR, b, :])
            link(ins)
            dve.wait_ge(s_const, 16 * 9)
            from_bn_stats()
            link(nc.vector.tensor_scalar(sweep_nbias[:], sweep_bias[:], -1.0, None, ALU.mult))
            group_norm()
            link(nc.vector.tensor_tensor(gn_t[:, 2, :], gn_var[:], gn_a[:], ALU.mult))
            to_pe(nc.vector.tensor_tensor(gn_t[:, 2, :], gn_t[:, 2, :], gn_a[:], ALU.mult))
            rsqrt(gn_t[:, 3, :], bank[7][:, 0:B])
            gw, gb, b1, b2 = (vecs[:, i:i + 1] for i in range(4))
            link(nc.vector.tensor_scalar(gn_t[:, 3, :], gn_t[:, 3, :], gw, None, ALU.mult))
            link(nc.vector.tensor_tensor(aff[:, 0, :], gn_a[:], gn_t[:, 3, :], ALU.mult))
            link(nc.vector.tensor_tensor(aff[:, 1, :], gn_c[:], gn_t[:, 3, :], ALU.mult))
            to_pe(nc.vector.tensor_scalar(aff[:, 1, :], aff[:, 1, :], gb, None, ALU.add))
            link(nc.vector.tensor_scalar(ffn1_b[:], bank[7][:, 0:B], b1, None, ALU.add))
            for b in range(B):
                link(nc.vector.tensor_scalar(ffn1_s[:, b, :], ffn1_w[:], aff[:, 0, b:b + 1], None, ALU.mult))
            link(nc.vector.tensor_scalar(a1[:], gn_a[:], 1.0, None, ALU.add))
            nc.vector.tensor_scalar(cb[:], gn_c[:], b2, None, ALU.add).then_inc(s_coef, 1)

            def ffn(layer, with_stats):
                base = B * CHUNKS * layer
                with dve.Fori(0, CHUNKS) as j:
                    for b in range(B):
                        dve.wait_ge(s_xs, j * B + (base + b + 1))
                        dve.wait_ge(s_dn, j * B + (base + b + 1))
                        xs = state[:, bass.ts(j, CR), b, :]
                        nc.vector.tensor_tensor(xs, bank[2 + b % 2].rearrange("p (r w) -> p r w", r=CR), xs,
                                                ALU.add).then_inc(s_sum, 1)
                        if with_stats:
                            dve.wait_ge(s_sum, j * B + (base + b + 1))
                            nc.vector.bn_stats(stats[:, b, j, :], xs).then_inc(s_dve, 1)
                if with_stats:
                    chain[0] += CHUNKS * B
                    dve.wait_ge(s_dve, chain[0])

            ffn(0, True)

            def sweep(n):
                layer, along, rev = sweeps[n]
                h0, r0, n0 = hbase(n), row_count(n), STEPS * n
                turning = n % 4 == 1
                nb = sweep_nbias[:, n:n + 1]

                if not rev:
                    dve.wait_ge(s_row, r0 + 1)
                    for c in range(2):
                        new = state[:, 0, 2 * c:2 * c + 2, :] if along == "H" else biased_row[:, 0, 2 * c:2 * c + 2, :]
                        nc.vector.tensor_copy(x_row[c][0][:, :, 2:2 + HALF], new).then_inc(s_h[c], 1)

                def step(i, k, c, ring=0):
                    par = slot(n, k)
                    dve.wait_ge(s_conv[c], i * 2 + (n0 + k))
                    if c == 0:
                        dve.wait_ge(s_row, i * 2 + (r0 + k + (0 if n % 4 == 3 else 1)))
                    ps = bank[2 * c + par][:, 0:2 * HALF].rearrange("p (b w) -> p b w", b=2)
                    br = biased_row[:, k, 2 * c:2 * c + 2, :]
                    new = turn_ring[:, ring, 1 - k, 2 * c:2 * c + 2, :] if turning else cells(n, c, i, k)
                    nc.vector.scalar_tensor_tensor(x_row[c][par][:, :, 2:2 + HALF], ps, nb, br,
                                                   ALU.max, ALU.add).then_inc(s_h[c], 1)
                    nc.vector.scalar_tensor_tensor(new, ps, nb, br, ALU.max, ALU.add).then_inc(s_new[c], 1)
                for c in range(2):
                    step(0, 1, c)
                if turning:
                    def pair(i, k, left):
                        if left is not None:
                            dve.wait_ge(s_turn[k], left)
                        for r in range(2):
                            for c in range(2):
                                step(i, r, c, k)
                    gone = 64 * (PAIRS // 2) * layer
                    pair(1, 1, gone if layer else None)
                    with dve.Fori(1, PAIRS // 2) as m:
                        for k in range(2):
                            pair(m * 2 + k, k, m * 64 + gone)
                else:
                    with dve.Fori(1, PAIRS) as i:
                        for k in range(2):
                            for c in range(2):
                                step(i, k, c)

            def add_residual(layer):
                for c in range(2):
                    dve.wait_ge(s_new[c], STEPS * 4 * (layer + 1))
                for j in range(CHUNKS):
                    dve.wait_ge(s_rld[j % RING], 16 * (CHUNKS // RING * layer + j // RING + 1))
                    for b in range(B):
                        rows = state[:, j * CR:(j + 1) * CR, b, :]
                        last = nc.vector.scalar_tensor_tensor(rows, rows, 1.0, res[:, j % RING, :, b * HALF:(b + 1) * HALF],
                                                              ALU.mult, ALU.add, accum_out=sums[:, 0, b, j:j + 1])
                    last.then_inc(s_add, 1)
                    if j == 0:
                        dve.wait_ge(s_add, CHUNKS * layer + 1)
                        nc.vector.tensor_scalar(minus_shift[:], sums[:, 0, :, 0], -1.0 / (CR * HALF), None,
                                                ALU.mult).then_inc(s_shift, 1)
                dve.wait_ge(s_add, CHUNKS * (layer + 1))
                dve.wait_ge(s_sqs, B * CHUNKS * (layer + 1))
                from_sums()

            from_bn_stats()
            for layer in range(2):
                group_norm()
                nc.vector.tensor_scalar(aff[:, 0, :], gn_c[:], sweep_bias[:, 4 * layer:4 * layer + 1], None,
                                        ALU.add).then_inc(s_coef, 1)
                for n in range(4 * layer, 4 * layer + 4):
                    sweep(n)
                add_residual(layer)

            group_norm()
            link(nc.vector.tensor_scalar(a1[:], gn_a[:], 1.0, None, ALU.add))
            nc.vector.tensor_scalar(cb[:], gn_c[:], vecs[:, 5:6], None, ALU.add).then_inc(s_coef, 1)

            def kv_sum(b, n, started):
                k = b % 2
                dve.wait_ge(s_sqr, n + 1)
                nc.vector.tensor_reduce(ssum[:, k, :], sq[:, k, :].rearrange("p (g e) -> p g e", e=HD),
                                        axis=AX.X, op=ALU.add).then_inc(s_ss, 1)

            def kv_scale(b, n, started, m):
                k = b % 2
                dve.wait_ge(s_sd, n + 1)
                if started or b >= 2:
                    dve.wait_ge(s_tl, n - 1)
                nc.vector.tensor_scalar(dev[:, k, :], sdev[:, k, :], EPS, None, ALU.add).then_inc(s_dv, 1)
                dve.wait_ge(s_dv, m + 1)
                d = dev[:, k, :].rearrange("p (g v h) -> p g v h", v=2, h=HQ)
                nc.vector.tensor_tensor(dprod[:, k, :].rearrange("p (g h) -> p g h", h=HQ), d[:, :, 0, :], d[:, :, 1, :],
                                        ALU.mult).then_inc(s_dv, 1)
                dve.wait_ge(s_dv, m + 2)
                nc.vector.reciprocal(rkv[:, k, :], dprod[:, k, :]).then_inc(s_ri, 1)
                dve.wait_ge(s_ri, n + 1)
                dve.wait_ge(s_kc, n + 1)
                v = gram_kv[:, b, :, 1, :, 0:HD - 1]
                by = rkv[:, k, :].rearrange("p (g h) -> p g h", h=HQ).unsqueeze(3).to_broadcast([P, 4, HQ, HD - 1])
                nc.vector.tensor_tensor(v, v, by, ALU.mult).then_inc(s_vs, 1)

            def kv_step(j, b, started):
                if started or b >= 1:
                    kv_scale((b - 1) % B, j * B + (b - 1), started or b >= 3, j * (2 * B) + 2 * (b - 1))
                kv_sum(b, j * B + b, started)

            for b in range(B):
                kv_step(0, b, False)
            with dve.Fori(1, CHUNKS) as j:
                for b in range(B):
                    kv_step(j, b, True)
            kv_scale(B - 1, B * CHUNKS - 1, True, 2 * (B * CHUNKS - 1))

            dve.wait_ge(s_gr, B * CHUNKS)
            for b in range(B):
                ins = nc.vector.tensor_tensor(gram_sb[:, b, :], bank[4][:, b * P:(b + 1) * P], gmask[:], ALU.mult)
            to_pe(ins)
            to_pe(nc.vector.tensor_copy(t1_sb, bank[0][:, 0:B * C]))
            to_pe(nc.vector.tensor_scalar(kvt_sb[0:C, :, :], bank[1][0:C, 0:B * C].rearrange("p (b n) -> p b n", b=B),
                                          1.0 / N_PIX, None, ALU.mult))
            for r in range(2):
                nc.vector.tensor_copy(ht_dup[0:C, :, r, :], bank[2][0:C, 0:B * C].rearrange("p (b n) -> p b n", b=B))
            to_pe(nc.vector.tensor_copy(ht_sb[0:C, :], bank[2][0:C, 0:B * C]))
            link(nc.vector.tensor_tensor(gt_sb, bank[3][:, 0:B * C].rearrange("p (b n) -> p b n", b=B),
                                         o1_t[:].unsqueeze(1).to_broadcast([P, B, C]), ALU.add))
            for r in range(2):
                ins = nc.vector.tensor_copy(gt_dup[0:C, :, r, :], gt_sb[0:C, :, :])
            to_pe(ins)
            nc.vector.tensor_scalar(ffn1_b[:], bank[0][:, 0:B], vecs[:, 4:5], None, ALU.add)
            for b in range(B):
                for q in range(2):
                    blk = slice(q * C, (q + 1) * C)
                    ins = nc.vector.tensor_scalar(ffn1_s[blk, b, blk], gt_sb[blk, b, :], gn_a[blk, b:b + 1], None, ALU.mult)
            ins.then_inc(s_coef, 1)
            ffn(1, False)


def kernel(**inputs):
    import concourse.bacc as _bacc
    from concourse.bass_utils import run_bass_kernel_spmd as _run
    f = {k: np.ascontiguousarray(v) for k, v in inputs.items()}
    B, C, H, W = f["x"].shape
    arrays = {}
    arrays["x"] = f["x"].reshape(B, C, H, W // 2, 2).transpose(4, 1, 2, 0, 3).reshape(2 * C, H, B * W // 2)
    l1 = [f[f"L1_conv_w_{d}"].transpose(1, 2, 0) for d in "durl"]
    l2 = [f[f"L2_conv_kernel_{d}"][:, 0].transpose(2, 1, 0) for d in ("td", "dt", "lr", "rl")]
    arrays["taps"] = np.stack(l1 + l2)
    zero = np.zeros((C,), np.float32)
    arrays["sbias"] = np.stack([np.tile(f[f"L1_conv_b_{d}"], 2) for d in "durl"] + [np.tile(zero, 2)] * 4, axis=1)
    arrays["w1t"] = f["L0_conv_w1"].T
    arrays["w2t"] = f["L0_conv_w2"].T
    arrays["o2t"] = f["L3_conv_o2_w"].T
    arrays["vecs"] = np.stack([np.tile(f[n], 2) for n in ("L0_conv_gn_w", "L0_conv_gn_b", "L0_conv_b1", "L0_conv_b2",
                                                          "L3_conv_o1_b", "L3_conv_o2_b")], axis=1)
    qkv_w, qkv_b = f["L3_conv_qkv_w"].reshape(8, 3, 8, C), f["L3_conv_qkv_b"].reshape(8, 3, 8)
    arrays["wq"] = qkv_w[:, 0].reshape(C, C)
    arrays["bq"] = qkv_b[:, 0].reshape(C, 1)
    arrays["kvt"] = qkv_w[:, 1:].transpose(1, 0, 2, 3).reshape(2 * C, C).T
    arrays["kvb"] = qkv_b[:, 1:].transpose(1, 0, 2).reshape(1, 2 * C)
    arrays["o1t"] = f["L3_conv_o1_w"].T
    ln = np.stack([f[f"L3_conv_{n}"].reshape(C) for n in ("kln_w", "kln_b", "vln_w", "vln_b")])
    arrays["ln_rows"] = np.broadcast_to(ln, (2 * C, 4, C))
    ch = np.arange(2 * C) % C
    e, i, same = ch[:, None] % 8, ch[None, :C] % 8, ch[:, None] // 8 == ch[None, :C] // 8
    weight = same & (e < 7) & (e == i)
    arrays["ln_pat"] = np.stack([weight * 1.0 - (same & (e < 7) & (i == 7)), same & (e == 7)], axis=1).astype(np.float32)
    arrays["gmask"] = (np.arange(2 * C)[:, None] // 8 == np.arange(2 * C)[None, :] // 8).astype(np.float32)
    arrays["gmats"] = np.stack([(ch[:, None] // g == ch[None, :] // g) / (2.0 * g) for g in (2, 8)]).astype(np.float32)
    arrays = {f"{k}_in": np.ascontiguousarray(v) for k, v in arrays.items()}

    nc = _bacc.Bacc("TRN2", target_bir_lowering=False, num_devices=1)
    D = {k[:-3]: nc.dram_tensor(k, v.shape, mybir.dt.from_np(v.dtype), kind="ExternalInput").ap() for k, v in arrays.items()}
    D["resid"] = nc.dram_tensor("resid", (H // 2, 2 * C, 2, B * W // 2), mybir.dt.float32).ap()
    out = nc.dram_tensor("out_y", (2 * C, H * B * W // 2), mybir.dt.float32, kind="ExternalOutput").ap()
    build_program(nc, D, out, None)
    r = _run(nc, [arrays], core_ids=[0])
    y = r.results[0]["out_y"].reshape(2, C, H // 2, 2, B, W // 2)
    return np.ascontiguousarray(y.transpose(4, 1, 2, 0, 5, 3)).reshape(B, C, H, W)
```

```python
import numpy as np
import concourse.bass as bass
from concourse import mybir
from contextlib import ExitStack


def build_program(nc, D, out):
    F32, F32R = mybir.dt.float32, mybir.dt.float32r
    ALU, ACT, AX = mybir.AluOpType, mybir.ActivationFunctionType, mybir.AxisListType
    B, C, H, W = 4, 64, 128, 128
    P = 2 * C
    HALF = W // 2
    ROW = B * HALF
    PAIRS = H // 2
    TAPS2 = 5
    PADDED = HALF + 4
    CR = 8
    CHUNKS = H // CR
    NT = CR * HALF
    WH = HALF // 2
    RING_ROWS = 64
    BIG, LOW = 32, 16
    UNITS = CHUNKS + H // LOW
    ADDS = CHUNKS + B * (H // LOW)
    SQ_PAIRS = 3
    SQS = B * (UNITS - SQ_PAIRS)
    WARM_STATS, WARM_BLOCK, WARM_SWEEP, WARM_TURN = 4, 5, 8, 16
    LAG = 3
    EPS = 1e-5
    HEADS, HD = 8, 8
    GROUPS = 8 * 2 * HEADS
    HQ = 2 * HEADS
    N_PIX = H * W

    sweeps = []
    for layer in (0, 1):
        sweeps += [(layer, "H", False), (layer, "H", True), (layer, "W", False), (layer, "W", True)]
    NS = len(sweeps)

    ctx = ExitStack()
    with ctx:
        def sb(name, shape, dt=F32):
            return ctx.enter_context(nc.sbuf_tensor(name, shape, dt))

        def sem(name):
            return ctx.enter_context(nc.semaphore(name))

        state = sb("state", [P, H, 2, B, WH])
        state_b = state[:].rearrange("p (hp s) g b w -> p hp s g b w", s=2)
        half_rows = state[:].rearrange("p h g b w -> p (h g) b w")
        res = sb("res", [P, RING_ROWS, B, WH])
        x_row = [[sb(f"x_row{c}{k}", [P, 2, PADDED]) for k in range(2)] for c in range(2)]
        biased_row = sb("biased_row", [P, 2, B, HALF])
        turn_ring = sb("turn_ring", [P, 2, 2, 2, B, WH])
        w_taps = sb("w_taps", [P, 2, TAPS2, P])
        sweep_bias = sb("sweep_bias", [P, NS])
        sweep_nbias = sb("sweep_nbias", [P, NS])
        gmats = sb("gmats", [P, 2, P])
        vecs = sb("vecs", [P, 6])
        stats = sb("stats", [P, B, CHUNKS, 6])
        sums = sb("sums", [P, 2, B, UNITS])
        minus_shift = sb("minus_shift", [P, B])
        mv = sb("mv", [P, B, 2])
        gn_mean = sb("gn_mean", [P, B])
        gn_var = sb("gn_var", [P, B])
        gn_a = sb("gn_a", [P, B])
        gn_c = sb("gn_c", [P, B])
        gn_t = sb("gn_t", [P, 4, B])
        a1 = sb("a1", [P, B])
        cb = sb("cb", [P, B])
        aff = sb("aff", [P, 2, B])
        eps_t = sb("eps_t", [P, 1])
        ffn1_w = sb("ffn1_w", [P, P])
        ffn2_w = sb("ffn2_w", [P, 2, P])
        ffn1_s = sb("ffn1_s", [P, B, P])
        ffn1_b = sb("ffn1_b", [P, B])
        hid = sb("hid", [P, 2, NT])
        ring = [0, res[:].rearrange("p r b w -> p (r b w)")]

        def in_ring(n):
            ring[0] += n
            assert ring[0] <= RING_ROWS * B * WH
            return ring[1][:, ring[0] - n:ring[0]]

        def slots(ap):
            return ap.rearrange("p (k n) -> p k n", k=2)

        y_st = slots(in_ring(2 * NT))
        sq = slots(in_ring(4 * NT))
        gram_kv = in_ring(4 * 2 * NT).rearrange("p (k g v h e) -> p k g v h e", k=4, v=2, h=HQ, e=HD)
        ssum = slots(in_ring(2 * GROUPS))
        sdev = slots(in_ring(2 * GROUPS))
        dev = slots(in_ring(2 * GROUPS))
        dprod = slots(in_ring(GROUPS))
        rkv = slots(in_ring(GROUPS))
        gram_sb = sq[:, 0, 0:4 * P].rearrange("p (b n) -> p b n", b=B)
        r_sb = sq[:, 1, 0:B * (P + 1)].rearrange("p (b n) -> p b n", b=B)
        kv_w = sb("kv_w", [P, 2 * P])
        bias_raw = sb("bias_raw", [C, P])
        bias_hi = sb("bias_hi", [C, P], F32R)
        bias_rows = sb("bias_rows", [P, 2, 2, 2, C], F32R)
        ones = sb("ones", [P, P], F32R)
        centre = sb("centre", [P, 32])
        ln_cols = sb("ln_cols", [C, 4])
        ln_pat = sb("ln_pat", [C, 2, P])
        uv = sb("uv", [C, 2, P])
        gmask = sb("gmask", [P, P])
        wq = sb("wq", [C, C])
        wq_t = sb("wq_t", [C, C])
        o1_t = sb("o1_t", [P, C])
        o1_dup = sb("o1_dup", [C, 2, C])
        o1_a = sb("o1_a", [P, B, C])
        bq = sb("bq", [C, 1])
        q_col = sb("q_col", [C, B])
        q_ext = sb("q_ext", [P, B, P + 1])
        v_o1 = sb("v_o1", [P, 2, C])

        BANK = 512
        pair = [ctx.enter_context(nc.psum_tensor(f"banks{2 * i}_{2 * i + 1}", [P, 2 * BANK], F32)) for i in range(4)]
        bank = [pair[i // 2][:, (i % 2) * BANK:(i % 2 + 1) * BANK] for i in range(8)]

        resid = D["resid"]

        x_loaded = [sem(f"x_loaded{j}") for j in range(CHUNKS)]
        consts_loaded = sem("consts_loaded")
        memory_set = sem("memory_set")
        small_operand_ready = sem("small_operand_ready")
        small_product_done = sem("small_product_done")
        variance_ready = sem("variance_ready")
        root_ready = sem("root_ready")
        dve_link = sem("dve_link")
        coefs_ready = sem("coefs_ready")
        ffn_up_done = sem("ffn_up_done")
        hidden_ready = sem("hidden_ready")
        x_scaled = sem("x_scaled")
        ffn_down_done = sem("ffn_down_done")
        ffn_added = sem("ffn_added")
        row_ready = [sem(f"row_ready{c}") for c in range(2)]
        row_stored = [sem(f"row_stored{c}") for c in range(2)]
        conv_done = [sem(f"conv_done{c}") for c in range(2)]
        biased_row_ready = sem("biased_row_ready")
        taps_loaded = [sem(f"taps_loaded{k}") for k in range(2)]
        pair_turned = [sem(f"pair_turned{k}") for k in range(2)]
        resid_stored = sem("resid_stored")
        chunk_stored = [sem(f"chunk_stored{j}") for j in range(CHUNKS)]
        upper_loaded = [sem(f"upper_loaded{k}") for k in range(RING_ROWS // BIG)]
        lower_loaded = [sem(f"lower_loaded{k}") for k in range(RING_ROWS // LOW)]
        resid_added = sem("resid_added")
        shift_ready = sem("shift_ready")
        squares_summed = sem("squares_summed")
        halves_crossed = [sem(f"halves_crossed{j}") for j in range(CHUNKS)]
        out_stored = sem("out_stored")
        y_staged = sem("y_staged")
        kv_done = sem("kv_done")
        kv_squared = sem("kv_squared")
        kv_copied = sem("kv_copied")
        group_sums_ready = sem("group_sums_ready")
        deviation_ready = sem("deviation_ready")
        scale_link = sem("scale_link")
        inverse_ready = sem("inverse_ready")
        v_scaled = sem("v_scaled")
        tails_ready = sem("tails_ready")
        gram_done = sem("gram_done")
        block3_consts_loaded = sem("block3_consts_loaded")

        block = ctx.enter_context(nc.Block())

        def squares_before(u):
            return CHUNKS + ((u + 1) // 2 if u < 2 * SQ_PAIRS else u - SQ_PAIRS)

        STEPS = H - 1

        def hbase(n):
            return sum(STEPS + (0 if rev else 1) for _, _, rev in sweeps[:n])

        def row_count(n):
            return sum(STEPS + (0 if (m % 4 == 3) else 1) for m in range(n))

        def row_of(rev, i, k):
            return (H - 1 - k) - 2 * i if rev else 2 * i + k

        def tile_of(j, b):
            return half_rows[:, bass.ts(j, 2 * CR), b, :]

        def by_halves(ap):
            return ap.rearrange("p b (g w) -> p g b w", g=2)

        def cells(n, images, i, k, g):
            _, along, rev = sweeps[n]
            if along == "H":
                return state[:, row_of(rev, i, k), :, images, :]
            s = (1 - k) if rev else k
            w = (HALF - 1 - g * WH) - i if rev else i - g * WH if g else i
            return state_b[:, :, s, g, images, w].rearrange("p h b -> p b h")

        def halves(n, i):
            return 1 - i // WH if sweeps[n][2] else i // WH

        def as_cells(n, ap):
            return by_halves(ap) if sweeps[n][1] == "H" else ap

        def slot(n, k):
            return (k + 1) % 2 if sweeps[n][2] else k

        @block.sync
        def _(sp):
            for j in range(CHUNKS):
                sp.dma_start(state[:, j * CR:(j + 1) * CR, :, :, :].rearrange("p r g b w -> p r (g b w)"),
                             D["x"][:, j * CR:(j + 1) * CR, :]).then_inc(x_loaded[j], 16)

            def store_residual_a(j):
                for q in range(2):
                    for r in range(2):
                        src = state[q * C:(q + 1) * C, :, :, :, :].rearrange(
                            "c (j hp r) g b w -> c j hp r (g b w)", r=2, hp=CR // 2)[:, j, :, r, :]
                        dst = resid.rearrange("(j hp) (r c) s n -> j r c s hp n", hp=CR // 2, r=2)[j, r, :, q, :, :]
                        sp.dma_start(dst, src).then_inc(resid_stored, 16)

            with sp.Fori(0, CHUNKS) as j:
                sp.wait_ge(ffn_added, j * B + B)
                store_residual_a(j)

            for layer in (0, 1):
                n = 4 * layer + 1
                sp.wait_ge(row_stored[0], STEPS * n + 1)
                sp.wait_ge(row_stored[1], STEPS * n + 1)
                sp.wait_ge(biased_row_ready, row_count(n) + 2)

                def turn(m, k):
                    hp = m * -2 + (PAIRS - 1 - k)
                    for s in range(2):
                        for q in range(2):
                            sp.dma_start(state_b[q * C:(q + 1) * C, hp, s, :, :, :],
                                         turn_ring[s * C:(s + 1) * C, k, q, :, :, :]).then_inc(pair_turned[k], 16)
                turn(0, 0)
                sp.wait_ge(row_stored[0], STEPS * n + 3)
                sp.wait_ge(row_stored[1], STEPS * n + 3)
                turn(0, 1)
                with sp.Fori(1, PAIRS // 2) as m:
                    for k in range(2):
                        sp.wait_ge(row_stored[0], m * 4 + (STEPS * n + 2 * k + 1))
                        sp.wait_ge(row_stored[1], m * 4 + (STEPS * n + 2 * k + 1))
                        turn(m, k)
                if layer == 0:
                    sp.wait_ge(resid_stored, 16 * 4 * CHUNKS)
                else:
                    for j in range(CHUNKS):
                        sp.wait_ge(chunk_stored[j], 16)
                def load_residual(row, rows, g, done):
                    at = row % RING_ROWS
                    for s in range(2):
                        sp.dma_start(res[:, at:at + rows, :, :].rearrange("p (hp s) b w -> p hp s (b w)", s=2)[:, :, s, :],
                                     resid.rearrange("hp p s n -> p hp s n")
                                     [:, row // 2:(row + rows) // 2, s, g * B * WH:(g + 1) * B * WH]).then_inc(done, 16)
                for u in range(H // BIG):
                    if u >= RING_ROWS // BIG:
                        sp.wait_ge(resid_added, layer * ADDS + (u - RING_ROWS // BIG + 1) * BIG // CR)
                    load_residual(u * BIG, BIG, 1, upper_loaded[u % (RING_ROWS // BIG)])
                for u in range(H // LOW):
                    if u < RING_ROWS // LOW:
                        sp.wait_ge(resid_added, layer * ADDS + (H - RING_ROWS + (u + 1) * LOW) // CR)
                    else:
                        sp.wait_ge(resid_added, layer * ADDS + CHUNKS + B * (u - RING_ROWS // LOW + 1))
                    load_residual(u * LOW, LOW, 0, lower_loaded[u % (RING_ROWS // LOW)])
                if layer == 0:
                    def cross(j):
                        sp.wait_ge(chunk_stored[j], 16)
                        sp.wait_ge(squares_summed, B * squares_before(j * CR // LOW + 1))
                        for q in range(2):
                            sp.dma_start(state_b[q * C:(q + 1) * C, j * CR // 2:(j + 1) * CR // 2, 1 - q, :, :, :]
                                         .rearrange("c hp g b w -> c hp (g b w)"),
                                         resid.rearrange("hp (r c) s n -> r c hp s n", r=2)
                                         [1 - q, :, j * CR // 2:(j + 1) * CR // 2, q, :]).then_inc(halves_crossed[j], 16)

                    for j in range(CHUNKS):
                        low = j * CR // LOW
                        sp.wait_ge(resid_added, CHUNKS + B * (low + 1))
                        sp.wait_ge(lower_loaded[low % (RING_ROWS // LOW)], 32 * (low * LOW // RING_ROWS + 1))
                        sp.dma_start(resid.rearrange("hp p s n -> p hp (s n)")[:, j * CR // 2:(j + 1) * CR // 2, :],
                                     state[:, j * CR:(j + 1) * CR, :, :, :].rearrange("p (hp s) g b w -> p hp (s g b w)", s=2)
                                     ).then_inc(chunk_stored[j], 16)
                        if j >= 2:
                            cross(j - 2)
                    cross(CHUNKS - 2)
                    cross(CHUNKS - 1)
            with sp.Fori(0, CHUNKS) as j:
                sp.wait_ge(ffn_added, j * B + (B * CHUNKS + B))
                sp.dma_start(out[:, bass.ts(j, CR * ROW)], state[:].rearrange("p (j r) g b w -> p j (r g b w)", r=CR)[:, j, :]
                             ).then_inc(out_stored, 16)
            sp.wait_ge(out_stored, 16 * CHUNKS)

        @block.gpsimd
        def _(pool):
            nc.gpsimd.memset(eps_t[:], EPS).then_inc(memory_set, 1)
            nc.gpsimd.memset(w_taps[:], 0.0).then_inc(memory_set, 1)
            nc.gpsimd.memset(ffn1_w[:], 0.0).then_inc(memory_set, 1)
            nc.gpsimd.memset(ffn2_w[:], 0.0).then_inc(memory_set, 1)
            for c in range(2):
                for k in range(2):
                    nc.gpsimd.memset(x_row[c][k][:], 0.0).then_inc(memory_set, 1)
            nc.gpsimd.memset(sums[:], 0.0).then_inc(memory_set, 1)
            nc.gpsimd.memset(kv_w[:], 0.0).then_inc(memory_set, 1)
            nc.gpsimd.memset(bias_raw[:], 0.0).then_inc(memory_set, 1)
            nc.gpsimd.memset(bias_rows[:].bitcast(F32), 0.0).then_inc(memory_set, 1)
            nc.gpsimd.memset(ones[:].bitcast(F32), 1.0).then_inc(memory_set, 1)

            def tails(b, n):
                k = b % 2
                pool.wait_ge(kv_copied, n + 1)
                pool.wait_ge(inverse_ready, n + 1)
                d = dev[:, k, :].rearrange("p (g v h) -> p g v h", v=2, h=HQ)
                nc.gpsimd.tensor_tensor(gram_kv[:, b, :, 0, :, HD - 1], d[:, :, 0, :],
                                        ones[:, 0:4 * HQ].bitcast(F32).rearrange("p (g h) -> p g h", h=HQ), ALU.mult)
                nc.gpsimd.tensor_tensor(gram_kv[:, b, :, 1, :, HD - 1], d[:, :, 1, :],
                                        rkv[:, k, :].rearrange("p (g h) -> p g h", h=HQ), ALU.mult).then_inc(tails_ready, 1)

            for b in range(B):
                tails(b, b)
            with pool.Fori(1, CHUNKS) as j:
                for b in range(B):
                    tails(b, j * B + b)

        @block.scalar
        def _(act):
            act.wait_ge(memory_set, 13)
            for dst, src in ((gmats[:], D["gmats"].rearrange("g p q -> p g q")), (vecs[:], D["vecs"]), (sweep_bias[:], D["sbias"])):
                act.dma_start(dst, src).then_inc(consts_loaded, 16)
            for q in range(2):
                blk = slice(q * C, (q + 1) * C)
                act.dma_start(ffn1_w[blk, blk], D["w1t"]).then_inc(consts_loaded, 16)
                act.dma_start(ffn2_w[blk, 0, blk], D["w2t"]).then_inc(consts_loaded, 16)
                act.dma_start(ffn2_w[blk, 1, blk], D["o2t"]).then_inc(consts_loaded, 16)

                act.dma_start(kv_w[:].rearrange("p (v q n) -> p v q n", v=2, q=2)[blk, :, q, :],
                              D["kvt"].rearrange("c (v n) -> c v n", v=2)).then_inc(block3_consts_loaded, 16)
                act.dma_start(bias_raw[32 * q:32 * q + 1, :], D["kvb"]).then_inc(block3_consts_loaded, 16)
                act.dma_start(o1_dup[:, q, :], D["o1t"]).then_inc(block3_consts_loaded, 16)
                act.dma_start(o1_t[blk, :], D["o1t"]).then_inc(block3_consts_loaded, 16)
            for dst, name in ((bq[:], "bq"), (ln_cols[:], "ln_cols"), (ln_pat[:], "ln_pat"), (gmask[:], "gmask"),
                              (wq[:], "wq"), (wq_t[:], "wqt")):
                act.dma_start(dst, D[name]).then_inc(block3_consts_loaded, 16)

            def load_taps(n):
                if n >= 2:
                    act.wait_ge(conv_done[1], STEPS * (n - 1))
                for q in range(2):
                    for r in range(2):
                        taps = [(s, 2 * s + q - r) for s in range(TAPS2) if 0 <= 2 * s + q - r <= 8]
                        s0, t0, cnt = taps[0][0], taps[0][1], len(taps)
                        act.dma_start(w_taps[q * C:(q + 1) * C, n % 2, s0:s0 + cnt, r * C:(r + 1) * C],
                                      D["taps"][n, :, t0:t0 + 2 * cnt - 1:2, :]).then_inc(taps_loaded[n % 2], 16)

            load_taps(0)

            def root(k):
                act.wait_ge(variance_ready, k)
                nc.scalar.activation(gn_t[:, 1, :], gn_var[:], ACT.Sqrt, bias=eps_t[:]).then_inc(root_ready, 1)

            root(1)
            root(2)

            def ffn(layer, func):
                base = B * CHUNKS * layer
                act.wait_ge(coefs_ready, 5 if layer else 1)
                def tile(j, b):
                    t = j * B + (b + base)
                    act.wait_ge(ffn_up_done, t + 1)
                    nc.scalar.activation(hid[:, b % 2, :], bank[b % 2], func, bias=ffn1_b[:, b:b + 1]).then_inc(hidden_ready, 1)
                    xs = tile_of(j, b)
                    nc.scalar.activation(xs, xs, ACT.Identity, scale=a1[:, b:b + 1], bias=cb[:, b:b + 1]).then_inc(x_scaled, 1)
                with act.Fori(0, CHUNKS) as j:
                    for b in range(B):
                        tile(j, b)

            ffn(0, ACT.Relu)

            def rows(n):
                layer, along, rev = sweeps[n]
                first, start = n % 4 == 0, row_count(n)
                if n + 1 < NS and n % 4 != 2:
                    load_taps(n + 1)
                if first:
                    root(3 + layer)
                    act.wait_ge(coefs_ready, 2 + layer)
                    if layer == 0:
                        act.wait_ge(resid_stored, 16 * 4 * CHUNKS)
                    else:
                        act.wait_ge(halves_crossed[0], 32)
                if n % 4 == 2:
                    for k in range(2):
                        act.wait_ge(pair_turned[k], 64 * (PAIRS // 2) * (layer + 1))
                elif n % 4 != 0:
                    act.wait_ge(row_stored[0], STEPS * n)
                    act.wait_ge(row_stored[1], STEPS * n)

                def row(i, k, g):
                    if first:
                        for b in range(B):
                            src = state[:, row_of(rev, i, k), :, b, :]
                            last = nc.scalar.activation(biased_row[:, k, b, :].rearrange("p (g w) -> p g w", g=2), src,
                                                        ACT.Identity, scale=gn_a[:, b:b + 1], bias=aff[:, 0, b:b + 1])
                        last.then_inc(biased_row_ready, 1)
                        return
                    nc.scalar.activation(as_cells(n, biased_row[:, k, :, :]), cells(n, slice(0, B), i, k, g), ACT.Identity,
                                         bias=sweep_bias[:, n:n + 1]).then_inc(biased_row_ready, 1)

                if first:
                    for b in range(B):
                        xs = state[:, 0, :, b, :]
                        last = nc.scalar.activation(xs, xs, ACT.Identity, scale=gn_a[:, b:b + 1], bias=gn_c[:, b:b + 1])
                    last.then_inc(biased_row_ready, 1)
                elif n % 4 == 1:
                    nc.scalar.activation(turn_ring[:, 0, 1, :, :, :], state[:, H - 1, :, :, :], ACT.Copy).then_inc(biased_row_ready, 1)
                elif n % 4 == 2:
                    nc.scalar.activation(biased_row[:, 0, :, :], cells(n, slice(0, B), 0, 0, 0), ACT.Copy).then_inc(biased_row_ready, 1)
                row(0, 1, halves(n, 0))
                if n % 4 == 2:
                    load_taps(n + 1)

                def next_row(i, k, g=0):
                    for c in range(2):
                        act.wait_ge(row_ready[c], i * 2 + (hbase(n) + k - 2 + (0 if rev else 1)))
                        if not isinstance(i, int) or STEPS * n + k:
                            act.wait_ge(row_stored[c], i * 2 + (STEPS * n + k - 2))
                    row(i, k, g)

                if n == 0:
                    next_row(1, 0)
                    next_row(1, 1)
                if n == 4:
                    for j in range(CHUNKS):
                        if j:
                            act.wait_ge(halves_crossed[j], 32)
                        with act.Fori(max(j * CR // 2, 1), (j + 1) * CR // 2) as i:
                            for k in range(2):
                                next_row(i, k)
                elif n % 4 == 3:
                    first_m = PAIRS // 4 + 1
                    for start, stop in ((1, WH), (WH, 2 * first_m)):
                        with act.Fori(start, stop) as i:
                            for k in range(2):
                                next_row(i, k, halves(n, start))
                    act.wait_ge(shift_ready, layer + 1)

                    def rows_and_squares(m):
                        for t in range(B):
                            next_row(m * 2 + t // 2, t % 2, 0)
                            if t == 0:
                                act.wait_ge(resid_added, m + (layer * ADDS - first_m + 1))
                            square(layer, m - first_m, t, m * B + (layer * SQS - B * first_m))
                    rows_and_squares(first_m)
                    with act.Fori(first_m + 1, PAIRS // 2) as m:
                        rows_and_squares(m)
                else:
                    for start, stop in ((2 if n == 0 else 1, WH), (WH, PAIRS)):
                        with act.Fori(start, stop) as i:
                            for k in range(2):
                                next_row(i, k, halves(n, start))

            def square(layer, j, b, before):
                if not (isinstance(before, int) and before == 0):
                    act.wait_ge(squares_summed, before + (b - B + 1))
                nc.scalar.activation(bank[4 + b][:, 0:CR * WH].rearrange("p (r w) -> p r w", r=CR),
                                     state[:, bass.ts(j, CR), 1, b, :], ACT.Square, bias=minus_shift[:, b:b + 1],
                                     accum_out=sums[:, 1, b, bass.ds(j, 1)]).then_inc(squares_summed, 1)

            def last_squares(layer):
                j = CHUNKS - 1
                act.wait_ge(resid_added, layer * ADDS + j + 1)
                for b in range(B):
                    square(layer, j, b, layer * SQS + B * j)
                count = B * (layer * (UNITS - SQ_PAIRS) + CHUNKS)
                for u, units in [(2 * m, 2) for m in range(SQ_PAIRS)] + [(m, 1) for m in range(2 * SQ_PAIRS, H // LOW)]:
                    at, rows_, unit = u * LOW, units * LOW, CHUNKS + u
                    for b in range(B):
                        act.wait_ge(resid_added, layer * ADDS + CHUNKS + B * (u + units - 1) + b + 1)
                        act.wait_ge(squares_summed, count - 1)
                        nc.scalar.activation(pair[2 + b % 2][:, 0:rows_ * WH].rearrange("p (r w) -> p r w", r=rows_),
                                             state[:, at:at + rows_, 0, b, :], ACT.Square, bias=minus_shift[:, b:b + 1],
                                             accum_out=sums[:, 1, b, unit:unit + 1]).then_inc(squares_summed, 1)
                        count += 1

            for n in range(4):
                rows(n)
            last_squares(0)
            for n in range(4, 8):
                rows(n)
            last_squares(1)
            root(5)
            act.wait_ge(coefs_ready, 4)

            def kv_root(k, n):
                act.wait_ge(group_sums_ready, n + 1)
                nc.scalar.activation(sdev[:, k, :], ssum[:, k, :], ACT.Sqrt, scale=1.0 / (HD - 1)).then_inc(deviation_ready, 1)

            def kv_square(b, n, started):
                k = b % 2
                act.wait_ge(kv_done, n + 1)
                if started or b >= 2:
                    act.wait_ge(group_sums_ready, n - 1)
                nc.scalar.activation(sq[:, k, :], pair[k][:], ACT.Square).then_inc(kv_squared, 1)
                if started:
                    act.wait_ge(gram_done, n - 3)
                nc.scalar.activation(gram_kv[:, b, :, :, :, :].rearrange("p g v h e -> p (g v h e)"), pair[k][:],
                                     ACT.Copy).then_inc(kv_copied, 1)

            def kv_stage(j, b, started, after_first=False):
                n = j * B + b
                if started or b >= 2:
                    act.wait_ge(kv_done, n - 1)
                nc.scalar.activation(y_st[:, b % 2, :].rearrange("p (r w) -> p r w", w=WH), tile_of(j, b),
                                     ACT.Identity, scale=gn_a[:, b:b + 1], bias=gn_c[:, b:b + 1]).then_inc(y_staged, 1)
                if started or b >= 1:
                    kv_square((b - 1) % B, n - 1, started and b >= 1 or after_first)
                if started or b >= 2:
                    kv_root(b % 2, n - 2)

            for m in range(2 * B):
                kv_stage(m // B, m % B, m >= B)
            with act.Fori(2, CHUNKS) as j:
                for b in range(B):
                    kv_stage(j, b, True, True)
            n = B * CHUNKS
            kv_square(B - 1, n - 1, True)
            kv_root(0, n - 2)
            kv_root(1, n - 1)
            ffn(1, ACT.Gelu)

        @block.tensor
        def _(pe):
            steps = [0]

            def stat_product(g, cols):
                steps[0] += 1
                pe.wait_ge(small_operand_ready, steps[0])
                nc.tensor.matmul(bank[7][:, 0:cols.shape[-1]], gmats[:, g, :], cols, start=True, stop=True).then_inc(small_product_done, 1)

            def keep_warm(products):
                for _ in range(products):
                    nc.tensor.matmul(bank[5][:, 0:P], gmats[:, 0, :], ones[:].bitcast(F32), start=True, stop=True)

            pe.wait_ge(consts_loaded, 16 * 9)
            stat_product(0, mv[:, :, 0])
            stat_product(0, gn_t[:, 3, :])
            stat_product(1, gn_t[:, 2, :])
            keep_warm(WARM_STATS)
            steps[0] += 1
            pe.wait_ge(small_operand_ready, steps[0])
            nc.tensor.matmul(bank[7][:, 0:B], ffn1_w[:], aff[:, 1, :], start=True, stop=True).then_inc(small_product_done, 1)
            keep_warm(WARM_BLOCK)

            def ffn(layer):
                base = B * CHUNKS * layer
                pe.wait_ge(coefs_ready, 5 if layer else 1)

                def up(j, b):
                    nc.tensor.matmul(bank[b % 2], ffn1_s[:, b, :], tile_of(j, b),
                                     start=True, stop=True).then_inc(ffn_up_done, 1)

                def down(b):
                    nc.tensor.matmul(bank[2 + b % 2], ffn2_w[:, layer, :], hid[:, b % 2, :],
                                     start=True, stop=True).then_inc(ffn_down_done, 1)

                def second(j, b, start):
                    pe.wait_ge(hidden_ready, j * B + (base + b + 1))
                    if b >= 2 or not start:
                        pe.wait_ge(ffn_added, j * B + (base + b - 1))
                    down(b)

                def chunk(j, start):
                    for b in range(B):
                        up(j, b)
                        if b:
                            second(j, b - 1, start)
                    second(j, B - 1, start)
                chunk(0, True)
                with pe.Fori(1, CHUNKS) as j:
                    chunk(j, False)

            ffn(0)

            def conv(n, c, k, hcount):
                par, src = slot(n, k), slot(n, 1 - k)
                out_ps = bank[2 * c + par][:, 0:2 * HALF].rearrange("p (b w) -> p b w", b=2)
                pe.wait_ge(row_ready[c], hcount)
                for s in range(TAPS2):
                    last = nc.tensor.matmul(out_ps, w_taps[:, n % 2, s, :], x_row[c][src][:, :, s:s + HALF],
                                            start=s == 0, stop=s == TAPS2 - 1)
                last.then_inc(conv_done[c], 1)

            def sweep(n):
                rev = sweeps[n][2]
                before = hbase(n) + (0 if rev else 1)
                pe.wait_ge(taps_loaded[n % 2], 64 * (n // 2 + 1))
                for c in range(2):
                    conv(n, c, 1, before)
                with pe.Fori(1, PAIRS) as i:
                    for k in range(2):
                        for c in range(2):
                            conv(n, c, k, i * 2 + (before + k - 1))

            for n in range(NS):
                if n % 4 == 0:
                    stat_product(0, mv[:, :, 0])
                    stat_product(0, gn_t[:, 3, :])
                    keep_warm(WARM_SWEEP)
                sweep(n)
                if n == 5:
                    steps[0] += 1
                    pe.wait_ge(small_operand_ready, steps[0])
                    nc.tensor.matmul(bank[6][:, 0:C], uv[:, 0, :], wq[:], start=True, stop=True)
                    nc.tensor.matmul(bank[6][:, C:2 * C], uv[:, 1, :], o1_t[0:C, :], start=True, stop=True).then_inc(small_product_done, 1)
                if n % 4 == 1:
                    keep_warm(WARM_TURN)
            stat_product(0, mv[:, :, 0])
            stat_product(0, gn_t[:, 3, :])
            steps[0] += 1
            pe.wait_ge(small_operand_ready, steps[0])
            nc.tensor.matmul(bank[7][0:C, 0:B], wq_t[:], gn_c[0:C, :], start=True, stop=True).then_inc(small_product_done, 1)
            steps[0] += 1
            pe.wait_ge(small_operand_ready, steps[0])
            nc.tensor.matmul(bank[7][:, 0:B], uv[:, 0, :], q_col[:], start=True, stop=True).then_inc(small_product_done, 1)
            keep_warm(WARM_BLOCK)

            def kv_products(j, b, started):
                k, n = b % 2, j * B + b
                pe.wait_ge(y_staged, n + 1)
                if started or b >= 2:
                    pe.wait_ge(kv_copied, n - 1)
                for u in range(2):
                    ps = pair[k][:, u * BANK:(u + 1) * BANK]
                    nc.tensor.matmul(ps, ones[:], bias_rows[:].rearrange("p t v q n -> p (t v q n)"), start=True, stop=False)
                    for t in range(2):
                        col = (2 * u + t) * P
                        last = nc.tensor.matmul(ps[:, t * 2 * P:(t + 1) * 2 * P], y_st[:, k, col:col + P], kv_w[:],
                                                start=False, stop=t == 1)
                last.then_inc(kv_done, 1)

            def gram(b, n):
                pe.wait_ge(v_scaled, n + 1)
                pe.wait_ge(tails_ready, n + 1)
                for t in range(4):
                    part = gram_kv[:, b, t, :, :, :].rearrange("p v h e -> p v (h e)")
                    last = nc.tensor.matmul(bank[4][:, b * P:(b + 1) * P], part[:, 0, :], part[:, 1, :],
                                            start=isinstance(n, int) and n == 0 and t == 0,
                                            stop=isinstance(n, int) and n >= B * (CHUNKS - 1) and t == 3, skip_group_check=True)
                last.then_inc(gram_done, 1)

            for b in range(B):
                kv_products(0, b, False)
                if b == B - 1:
                    gram(0, 0)
            with pe.Fori(1, CHUNKS) as j:
                for b in range(B):
                    kv_products(j, b, True)
                    gram((b - LAG) % B, j * B + (b - LAG))
            for m in range(B * CHUNKS - LAG, B * CHUNKS):
                gram(m % B, m)

            def operands():
                steps[0] += 1
                pe.wait_ge(small_operand_ready, steps[0])

            nc.tensor.matmul(bank[3][:, 0:B], o1_dup[:].rearrange("p r n -> p (r n)"), gn_c[0:C, :], start=True, stop=False)
            operands()
            for b in range(B):
                at = b // 2 * BANK + b % 2 * (P + 1)
                last = nc.tensor.matmul(pair[0][:, at:at + P + 1], gram_sb[:, b, :], q_ext[:, b, :], start=True, stop=True)
            last.then_inc(small_product_done, 1)
            operands()
            for b in range(B):
                nc.tensor.matmul(bank[2][:, b * C:(b + 1) * C], r_sb[:, b, 0:P], v_o1[:, 0, :], start=True, stop=True)
            nc.tensor.matmul(bank[3][:, 0:B], v_o1[:].rearrange("p r n -> p (r n)"), r_sb[:, :, P], start=False,
                             stop=True).then_inc(small_product_done, 1)
            keep_warm(WARM_BLOCK)
            ffn(1)

        @block.vector
        def _(dve):
            chain = [0]

            def link(ins):
                chain[0] += 1
                ins.then_inc(dve_link, 1)
                dve.wait_ge(dve_link, chain[0])

            gp, gq, rt = [0], [0], [0]

            def to_pe(ins):
                ins.then_inc(small_operand_ready, 1)
                gq[0] += 1
                dve.wait_ge(small_product_done, gq[0])

            def rsqrt(dst, var):
                nc.vector.tensor_copy(gn_var[:], var).then_inc(variance_ready, 1)
                rt[0] += 1
                dve.wait_ge(root_ready, rt[0])
                link(nc.vector.reciprocal(dst, gn_t[:, 1, :]))

            def from_bn_stats():
                for b in range(B):
                    ins = nc.vector.bn_aggr(mv[:, b, :], stats[:, b, :, :].rearrange("p j s -> p (j s)"))
                to_pe(ins)

            def from_sums():
                n = CR * HALF * CHUNKS
                link(nc.vector.tensor_reduce(gn_t[:, 2:4, :], sums[:], axis=AX.X, op=ALU.add))
                link(nc.vector.tensor_scalar(gn_t[:, 2:4, :], gn_t[:, 2:4, :], 1.0 / n, None, ALU.mult))
                nc.vector.tensor_copy(mv[:, :, 0], gn_t[:, 2, :])
                link(nc.vector.tensor_tensor(gn_t[:, 0, :], gn_t[:, 2, :], minus_shift[:], ALU.add))
                link(nc.vector.tensor_tensor(gn_t[:, 0, :], gn_t[:, 0, :], gn_t[:, 0, :], ALU.mult))
                to_pe(nc.vector.tensor_tensor(mv[:, :, 1], gn_t[:, 3, :], gn_t[:, 0, :], ALU.subtract))

            def group_norm():
                link(nc.vector.tensor_copy(gn_mean[:], bank[7][:, 0:B]))
                link(nc.vector.tensor_tensor(gn_t[:, 0, :], mv[:, :, 0], gn_mean[:], ALU.subtract))
                link(nc.vector.tensor_tensor(gn_t[:, 0, :], gn_t[:, 0, :], gn_t[:, 0, :], ALU.mult))
                to_pe(nc.vector.tensor_tensor(gn_t[:, 3, :], gn_t[:, 0, :], mv[:, :, 1], ALU.add))
                rsqrt(gn_a[:], bank[7][:, 0:B])
                link(nc.vector.scalar_tensor_tensor(gn_c[:], gn_mean[:], -1.0, gn_a[:], ALU.mult, ALU.mult))

            def centre_kv_weights():
                dve.wait_ge(memory_set, 13)
                dve.wait_ge(block3_consts_loaded, 16 * 14)
                for w, rows_, g in ((kv_w, P, 32), (bias_raw, C, 16)):
                    v = w[:].rearrange("p (g e) -> p g e", e=HD)
                    m = centre[0:rows_, 0:g]
                    link(nc.vector.tensor_reduce(m, v, axis=AX.X, op=ALU.add))
                    link(nc.vector.tensor_scalar(m, m, 1.0 / HD, None, ALU.mult))
                    link(nc.vector.tensor_tensor(v, v, m.unsqueeze(2).to_broadcast([rows_, g, HD]), ALU.subtract))
                link(nc.vector.tensor_copy(bias_hi[:], bias_raw[:]))
                by_kv = bias_raw[:].rearrange("p (v n) -> p v n", v=2)
                hi_kv = bias_hi[:].bitcast(F32).rearrange("p (v n) -> p v n", v=2)
                for t in range(2):
                    for q in range(2):
                        nc.vector.tensor_copy(bias_rows[0:1, t, :, q, :], by_kv[0:1, :, :])
                        nc.vector.tensor_tensor(bias_rows[32:33, t, :, q, :], by_kv[32:33, :, :], hi_kv[32:33, :, :], ALU.subtract)
            def layernorm_affines():
                for v in range(2):
                    ins = nc.vector.tensor_scalar(uv[:, v, :], ln_pat[:, 0, :], ln_cols[:, 2 * v:2 * v + 1], None, ALU.mult)
                link(ins)
                for v in range(2):
                    ins = nc.vector.scalar_tensor_tensor(uv[:, v, :], ln_pat[:, 1, :], ln_cols[:, 2 * v + 1:2 * v + 2],
                                                         uv[:, v, :], ALU.mult, ALU.add)
                to_pe(ins)
                for r in range(2):
                    nc.vector.tensor_scalar(v_o1[:, r, :], bank[6][:, C:2 * C], 1.0 / N_PIX, None, ALU.mult)
                    for b in range(B):
                        ins = nc.vector.tensor_copy(q_ext[:, b, r * C:(r + 1) * C], bank[6][:, 0:C])
                link(ins)

            for j in range(CHUNKS):
                dve.wait_ge(x_loaded[j], 16)
                for b in range(B):
                    ins = nc.vector.bn_stats(stats[:, b, j, :], tile_of(j, b))
            link(ins)
            dve.wait_ge(consts_loaded, 16 * 9)
            from_bn_stats()
            link(nc.vector.tensor_scalar(sweep_nbias[:], sweep_bias[:], -1.0, None, ALU.mult))
            group_norm()
            link(nc.vector.tensor_tensor(gn_t[:, 2, :], gn_var[:], gn_a[:], ALU.mult))
            to_pe(nc.vector.tensor_tensor(gn_t[:, 2, :], gn_t[:, 2, :], gn_a[:], ALU.mult))
            rsqrt(gn_t[:, 3, :], bank[7][:, 0:B])
            gw, gb, b1, b2 = (vecs[:, i:i + 1] for i in range(4))
            link(nc.vector.tensor_scalar(gn_t[:, 3, :], gn_t[:, 3, :], gw, None, ALU.mult))
            link(nc.vector.tensor_tensor(aff[:, 0, :], gn_a[:], gn_t[:, 3, :], ALU.mult))
            link(nc.vector.tensor_tensor(aff[:, 1, :], gn_c[:], gn_t[:, 3, :], ALU.mult))
            to_pe(nc.vector.tensor_scalar(aff[:, 1, :], aff[:, 1, :], gb, None, ALU.add))
            link(nc.vector.tensor_scalar(ffn1_b[:], bank[7][:, 0:B], b1, None, ALU.add))
            for b in range(B):
                nc.vector.tensor_scalar(ffn1_s[:, b, :], ffn1_w[:], aff[:, 0, b:b + 1], None, ALU.mult)
            link(nc.vector.tensor_scalar(a1[:], gn_a[:], 1.0, None, ALU.add))
            nc.vector.tensor_scalar(cb[:], gn_c[:], b2, None, ALU.add).then_inc(coefs_ready, 1)

            def ffn(layer, with_stats):
                base = B * CHUNKS * layer
                with dve.Fori(0, CHUNKS) as j:
                    for b in range(B):
                        dve.wait_ge(x_scaled, j * B + (base + b + 1))
                        dve.wait_ge(ffn_down_done, j * B + (base + b + 1))
                        xs = tile_of(j, b)
                        nc.vector.tensor_tensor(xs, bank[2 + b % 2].rearrange("p (r w) -> p r w", w=WH), xs,
                                                ALU.add).then_inc(ffn_added, 1)
                        if with_stats:
                            dve.wait_ge(ffn_added, j * B + (base + b + 1))
                            nc.vector.bn_stats(stats[:, b, j, :], xs).then_inc(dve_link, 1)
                if with_stats:
                    chain[0] += CHUNKS * B
                    dve.wait_ge(dve_link, chain[0])

            ffn(0, True)

            def sweep(n):
                layer, along, rev = sweeps[n]
                r0, n0 = row_count(n), STEPS * n
                turning = n % 4 == 1
                nb = sweep_nbias[:, n:n + 1]

                if not rev:
                    dve.wait_ge(biased_row_ready, r0 + 1)
                    for c in range(2):
                        new = state[:, 0, :, 2 * c:2 * c + 2, :] if along == "H" else biased_row[:, 0, 2 * c:2 * c + 2, :]
                        nc.vector.tensor_copy(as_cells(n, x_row[c][0][:, :, 2:2 + HALF]), new).then_inc(row_ready[c], 1)

                def step(i, k, c, g, ring=0):
                    par = slot(n, k)
                    dve.wait_ge(conv_done[c], i * 2 + (n0 + k))
                    if c == 0:
                        dve.wait_ge(biased_row_ready, i * 2 + (r0 + k + (0 if n % 4 == 3 else 1)))
                    ps = bank[2 * c + par][:, 0:2 * HALF].rearrange("p (b w) -> p b w", b=2)
                    br = biased_row[:, k, 2 * c:2 * c + 2, :]
                    nc.vector.scalar_tensor_tensor(x_row[c][par][:, :, 2:2 + HALF], ps, nb, br,
                                                   ALU.max, ALU.add).then_inc(row_ready[c], 1)
                    if along == "W":
                        last = nc.vector.scalar_tensor_tensor(cells(n, slice(2 * c, 2 * c + 2), i, k, g), ps, nb, br,
                                                              ALU.max, ALU.add)
                    else:
                        for b in range(2):
                            im = 2 * c + b
                            new = turn_ring[:, ring, 1 - k, :, im, :] if turning else cells(n, im, i, k, g)
                            last = nc.vector.scalar_tensor_tensor(new, ps[:, b, :].rearrange("p (g w) -> p g w", g=2), nb,
                                                                  br[:, b, :].rearrange("p (g w) -> p g w", g=2),
                                                                  ALU.max, ALU.add)
                    last.then_inc(row_stored[c], 1)
                for c in range(2):
                    step(0, 1, c, halves(n, 0))
                if turning:
                    def turned_pair(i, k, left):
                        if left is not None:
                            dve.wait_ge(pair_turned[k], left)
                        for r in range(2):
                            for c in range(2):
                                step(i, r, c, 0, k)
                    gone = 64 * (PAIRS // 2) * layer
                    turned_pair(1, 1, gone if layer else None)
                    with dve.Fori(1, PAIRS // 2) as m:
                        for k in range(2):
                            turned_pair(m * 2 + k, k, m * 64 + gone)
                elif n % 4 == 3:
                    mid = PAIRS // 4
                    with dve.Fori(1, 2 * mid) as i:
                        for k in range(2):
                            for c in range(2):
                                step(i, k, c, halves(n, 1))
                    for c in range(2):
                        dve.wait_ge(row_stored[c], n0 + 4 * mid - 1)

                    def steps_and_chunk(m, ring_from):
                        for t in range(B):
                            for c in range(2):
                                step(m * 2 + t // 2, t % 2, c, 0)
                            j = m - mid
                            rows = state[:, bass.ts(j, CR), 1, t, :]
                            last = nc.vector.scalar_tensor_tensor(rows, rows, 1.0, res[:, bass.ts(m - ring_from, CR), t, :],
                                                                  ALU.mult, ALU.add, accum_out=sums[:, 0, t, bass.ds(j, 1)])
                        last.then_inc(resid_added, 1)

                    per, ring_slots = BIG // CR, RING_ROWS // BIG
                    for u in range(H // BIG):
                        dve.wait_ge(upper_loaded[u % ring_slots], 32 * (H // RING_ROWS * layer + u // ring_slots + 1))
                        start, ring_from = mid + u * per, mid + u // ring_slots * ring_slots * per
                        if u == 0:
                            steps_and_chunk(start, ring_from)
                            dve.wait_ge(resid_added, ADDS * layer + 1)
                            nc.vector.tensor_scalar(minus_shift[:], sums[:, 0, :, 0], -1.0 / (CR * WH), None,
                                                    ALU.mult).then_inc(shift_ready, 1)
                            start += 1
                        with dve.Fori(start, mid + (u + 1) * per) as m:
                            steps_and_chunk(m, ring_from)
                else:
                    for start, stop in ((1, WH), (WH, PAIRS)):
                        with dve.Fori(start, stop) as i:
                            for k in range(2):
                                for c in range(2):
                                    step(i, k, c, halves(n, start))

            def add_residual(layer):
                for c in range(2):
                    dve.wait_ge(row_stored[c], STEPS * 4 * (layer + 1))
                for u in range(H // LOW):
                    dve.wait_ge(lower_loaded[u % (RING_ROWS // LOW)], 32 * (H // RING_ROWS * layer + u * LOW // RING_ROWS + 1))
                    at = u * LOW
                    for b in range(B):
                        rows = state[:, at:at + LOW, 0, b, :]
                        nc.vector.scalar_tensor_tensor(rows, rows, 1.0, res[:, at % RING_ROWS:at % RING_ROWS + LOW, b, :],
                                                       ALU.mult, ALU.add,
                                                       accum_out=sums[:, 0, b, CHUNKS + u:CHUNKS + u + 1]).then_inc(resid_added, 1)
                dve.wait_ge(resid_added, ADDS * (layer + 1))
                dve.wait_ge(squares_summed, SQS * (layer + 1))
                from_sums()

            from_bn_stats()
            for layer in range(2):
                group_norm()
                nc.vector.tensor_scalar(aff[:, 0, :], gn_c[:], sweep_bias[:, 4 * layer:4 * layer + 1], None,
                                        ALU.add).then_inc(coefs_ready, 1)
                for n in range(4 * layer, 4 * layer + 4):
                    if n == 2:
                        centre_kv_weights()
                    if n == 6:
                        layernorm_affines()
                    sweep(n)
                add_residual(layer)

            group_norm()
            link(nc.vector.tensor_scalar(a1[:], gn_a[:], 1.0, None, ALU.add))
            nc.vector.tensor_scalar(cb[:], gn_c[:], vecs[:, 5:6], None, ALU.add).then_inc(coefs_ready, 1)
            for b in range(B):
                ins = nc.vector.tensor_scalar(o1_a[:, b, :], o1_t[:], gn_a[:, b:b + 1], None, ALU.mult)
            to_pe(ins)
            to_pe(nc.vector.tensor_scalar(q_col[:], bank[7][0:C, 0:B], bq[:], None, ALU.add))
            link(nc.vector.tensor_copy(q_ext[:, :, P], bank[7][:, 0:B]))

            def kv_sum(b, n):
                k = b % 2
                dve.wait_ge(kv_squared, n + 1)
                nc.vector.tensor_reduce(ssum[:, k, :], sq[:, k, :].rearrange("p (g e) -> p g e", e=HD),
                                        axis=AX.X, op=ALU.add).then_inc(group_sums_ready, 1)

            def kv_scale(b, n, started, m):
                k = b % 2
                dve.wait_ge(deviation_ready, n + 1)
                if started or b >= 2:
                    dve.wait_ge(tails_ready, n - 1)
                nc.vector.tensor_scalar(dev[:, k, :], sdev[:, k, :], EPS, None, ALU.add).then_inc(scale_link, 1)
                dve.wait_ge(scale_link, m + 1)
                d = dev[:, k, :].rearrange("p (g v h) -> p g v h", v=2, h=HQ)
                nc.vector.tensor_tensor(dprod[:, k, :].rearrange("p (g h) -> p g h", h=HQ), d[:, :, 0, :], d[:, :, 1, :],
                                        ALU.mult).then_inc(scale_link, 1)
                dve.wait_ge(scale_link, m + 2)
                nc.vector.reciprocal(rkv[:, k, :], dprod[:, k, :]).then_inc(inverse_ready, 1)
                dve.wait_ge(inverse_ready, n + 1)
                dve.wait_ge(kv_copied, n + 1)
                v = gram_kv[:, b, :, 1, :, 0:HD - 1]
                by = rkv[:, k, :].rearrange("p (g h) -> p g h", h=HQ).unsqueeze(3).to_broadcast([P, 4, HQ, HD - 1])
                nc.vector.tensor_tensor(v, v, by, ALU.mult).then_inc(v_scaled, 1)

            def kv_step(j, b, started):
                kv_sum(b, j * B + b)
                if started or b >= 1:
                    kv_scale((b - 1) % B, j * B + (b - 1), started or b >= 3, j * (2 * B) + 2 * (b - 1))

            for b in range(B):
                kv_step(0, b, False)
            with dve.Fori(1, CHUNKS) as j:
                for b in range(B):
                    kv_step(j, b, True)
            kv_scale(B - 1, B * CHUNKS - 1, True, 2 * (B * CHUNKS - 1))

            dve.wait_ge(gram_done, B * CHUNKS)
            for b in range(B):
                ins = nc.vector.tensor_tensor(gram_sb[:, b, :], bank[4][:, b * P:(b + 1) * P], gmask[:], ALU.mult)
            to_pe(ins)
            to_pe(nc.vector.tensor_copy(r_sb.rearrange("p (u b) n -> p u (b n)", u=2),
                                        pair[0][:].rearrange("p (u n) -> p u n", u=2)[:, :, 0:2 * (P + 1)]))
            nc.vector.tensor_scalar(ffn1_b[:], bank[3][:, 0:B], vecs[:, 4:5], None, ALU.add)
            for b in range(B):
                for q in range(2):
                    blk = slice(q * C, (q + 1) * C)
                    ins = nc.vector.scalar_tensor_tensor(ffn1_s[blk, b, blk], bank[2][blk, b * C:(b + 1) * C], gn_a[blk, b:b + 1],
                                                         o1_a[blk, b, :], ALU.mult, ALU.add)
            ins.then_inc(coefs_ready, 1)
            ffn(1, False)


def kernel(**inputs):
    import concourse.bacc as _bacc
    from concourse.bass_utils import run_bass_kernel_spmd as _run
    f = {k: np.ascontiguousarray(v) for k, v in inputs.items()}
    B, C, H, W = f["x"].shape
    arrays = {}
    arrays["x"] = f["x"].reshape(B, C, H, 2, W // 4, 2).transpose(5, 1, 2, 3, 0, 4).reshape(2 * C, H, B * W // 2)
    l1 = [f[f"L1_conv_w_{d}"].transpose(1, 2, 0) for d in "durl"]
    l2 = [f[f"L2_conv_kernel_{d}"][:, 0].transpose(2, 1, 0) for d in ("td", "dt", "lr", "rl")]
    arrays["taps"] = np.stack(l1 + l2)
    zero = np.zeros((C,), np.float32)
    arrays["sbias"] = np.stack([np.tile(f[f"L1_conv_b_{d}"], 2) for d in "durl"] + [np.tile(zero, 2)] * 4, axis=1)
    arrays["w1t"] = f["L0_conv_w1"].T
    arrays["w2t"] = f["L0_conv_w2"].T
    arrays["o2t"] = f["L3_conv_o2_w"].T
    arrays["vecs"] = np.stack([np.tile(f[n], 2) for n in ("L0_conv_gn_w", "L0_conv_gn_b", "L0_conv_b1", "L0_conv_b2",
                                                          "L3_conv_o1_b", "L3_conv_o2_b")], axis=1)
    qkv_w, qkv_b = f["L3_conv_qkv_w"].reshape(8, 3, 8, C), f["L3_conv_qkv_b"].reshape(8, 3, 8)
    arrays["wq"] = qkv_w[:, 0].reshape(C, C)
    arrays["bq"] = qkv_b[:, 0].reshape(C, 1)
    arrays["kvt"] = qkv_w[:, 1:].transpose(1, 0, 2, 3).reshape(2 * C, C).T
    arrays["kvb"] = qkv_b[:, 1:].transpose(1, 0, 2).reshape(1, 2 * C)
    arrays["o1t"] = f["L3_conv_o1_w"].T
    ln = np.stack([f[f"L3_conv_{n}"].reshape(C) for n in ("kln_w", "kln_b", "vln_w", "vln_b")])
    arrays["ln_cols"] = ln.T
    arrays["wqt"] = arrays["wq"].T
    ch = np.arange(2 * C) % C
    i, e, same = ch[:C, None] % 8, ch[None, :] % 8, ch[:C, None] // 8 == ch[None, :] // 8
    weight = same & (e < 7) & (e == i)
    arrays["ln_pat"] = np.stack([weight * 1.0 - (same & (e < 7) & (i == 7)), same & (e == 7)], axis=1).astype(np.float32)
    arrays["gmask"] = (np.arange(2 * C)[:, None] // 8 == np.arange(2 * C)[None, :] // 8).astype(np.float32)
    arrays["gmats"] = np.stack([(ch[:, None] // g == ch[None, :] // g) / (2.0 * g) for g in (2, 8)]).astype(np.float32)
    arrays = {f"{k}_in": np.ascontiguousarray(v) for k, v in arrays.items()}

    nc = _bacc.Bacc("TRN2", target_bir_lowering=False, num_devices=1)
    D = {k[:-3]: nc.dram_tensor(k, v.shape, mybir.dt.from_np(v.dtype), kind="ExternalInput").ap() for k, v in arrays.items()}
    D["resid"] = nc.dram_tensor("resid", (H // 2, 2 * C, 2, B * W // 2), mybir.dt.float32).ap()
    out = nc.dram_tensor("out_y", (2 * C, H * B * W // 2), mybir.dt.float32, kind="ExternalOutput").ap()
    build_program(nc, D, out)
    r = _run(nc, [arrays], core_ids=[0])
    y = r.results[0]["out_y"].reshape(2, C, H // 2, 2, 2, B, W // 4)
    return np.ascontiguousarray(y.transpose(5, 1, 2, 0, 4, 6, 3)).reshape(B, C, H, W)
```
